# Optimizing a Trainium2 kernel written in Bass

```python
import numpy as np
import jax
import jax.numpy as jnp

def _softmax(x, axis=-1):
    return jax.nn.softmax(x, axis=axis)

def _gelu(x):
    return jax.nn.gelu(x, approximate=True)

def _silu(x):
    return jax.nn.silu(x)

def _sigmoid(x):
    return jax.nn.sigmoid(x)

def _layernorm(x, axis=-1, eps=1e-05):
    m = jnp.mean(x, axis=axis, keepdims=True)
    v = jnp.var(x, axis=axis, keepdims=True)
    return (x - m) / jnp.sqrt(v + eps)

def _scatter_add(tgt, idx, src, axis=0):
    return tgt.at[idx].add(src)

def _segment_sum(src, seg, n):
    return jax.ops.segment_sum(src, seg, n)
kernel_name = 'mk_flamingo_gated_d2_seqx_r8_afccbd'

def setup_inputs(seed: int=0):
    np.random.seed(seed)
    _w = jnp.asarray

    def _rec_inputs():
        import jax
        import jax.numpy as jnp
        _rk = jax.random.key(seed)
        x = -0.0002928 + 1 * jax.random.normal(jax.random.fold_in(_rk, 1), (32, 56, 128), jnp.float32)
        _lenS = 56 - jax.random.randint(jax.random.fold_in(_rk, 7), (32,), 0, max(1, 56 // 4) + 1, jnp.int32)
        _lenS2 = 1500 - jax.random.randint(jax.random.fold_in(_rk, 8), (32,), 0, max(1, 1500 // 4) + 1, jnp.int32)
        _ctx_1024P = jax.random.normal(jax.random.fold_in(_rk, 11), (32, 16, 128), jnp.float32)
        _ctx_1024c = jax.random.dirichlet(jax.random.fold_in(_rk, 511), 0.3 * jnp.ones((16,), jnp.float32), (32, 1500))
        _ctx_1024t = jnp.einsum('bsk,bkd->bsd', _ctx_1024c, _ctx_1024P)
        _ctx_1024t = _ctx_1024t * jax.lax.rsqrt(jnp.mean(jnp.square(_ctx_1024t)) + 1e-12) * 0.953939
        ctx_1024 = -1.39393e-06 + 0.999914 * (_ctx_1024t + 0.3 * jax.random.normal(jax.random.fold_in(_rk, 611), (32, 1500, 128), jnp.float32))
        _validS = jnp.arange(56)[None, :] < _lenS[:, None]
        _validS2 = jnp.arange(1500)[None, :] < _lenS2[:, None]
        _causal = jnp.tril(jnp.ones((56, 56), dtype=bool))
        mask_BxSxS2_if1 = jnp.where(jnp.ones((32, 56, 1500), dtype=bool), 1, 0).astype(jnp.int32)
        _g = jax.random.normal(jax.random.fold_in(_rk, 9001), (2, 2), jnp.float32)
        _g = jnp.sign(_g) * jnp.maximum(jnp.abs(_g), 1.0) + (_g == 0) * 1.0
        g_xattn = _g[0]
        g_ffn = _g[1]
        return (x, ctx_1024, mask_BxSxS2_if1, g_xattn, g_ffn)
    x, ctx_1024, mask_BxSxS2_if1, g_xattn, g_ffn = _rec_inputs()

    def _L0_xattn_setup():
        import jax, jax.numpy as jnp
        import numpy as np
        B, S, D, H = (2, 256, 128, 16)
        DH = D // H
        key = jax.random.key(seed)
        ks = jax.random.split(key, 12)
        sc = 0.02
        return {'query': jax.random.normal(ks[0], (B, S, D), jnp.float32), 'key': jax.random.normal(ks[1], (B, S, D), jnp.float32), 'value': jax.random.normal(ks[2], (B, S, D), jnp.float32), 'mask': jnp.ones((B, S, S), jnp.int32), 'qw': jax.random.normal(ks[3], (D, D), jnp.float32) * sc, 'qb': jnp.zeros((D,), jnp.float32), 'kw': jax.random.normal(ks[4], (D, D), jnp.float32) * sc, 'kb': jnp.zeros((D,), jnp.float32), 'vw': jax.random.normal(ks[5], (D, D), jnp.float32) * sc, 'vb': jnp.zeros((D,), jnp.float32), 'ow': jax.random.normal(ks[6], (D, D), jnp.float32) * sc, 'ob': jnp.zeros((D,), jnp.float32)}
    _L0_xattn_all = _L0_xattn_setup()
    _L0_xattn_in = {k: v for k, v in _L0_xattn_all.items() if k in ('qw', 'qb', 'kw', 'kb', 'vw', 'vb', 'ow', 'ob')}
    del _L0_xattn_all

    def _L0_ffn_setup():
        import jax, jax.numpy as jnp
        import numpy as np
        B, T, C = (2, 256, 128)
        H, D = (16, 64)
        CR = 8
        R = C // CR
        ROPE = D // 2
        NOPE = D - ROPE
        E, K, I, S = (8, 2, 64, 1)
        THETA = 100000.0
        EPS = 1e-05

        def _rmsnorm(x, w):
            rms = jnp.sqrt(jnp.mean(x * x, axis=-1, keepdims=True) + EPS)
            return w * (x / rms)

        def _rope(xh):
            d = xh.shape[-1]
            t = jnp.arange(xh.shape[2], dtype=jnp.float32)
            freqs = 1.0 / THETA ** (jnp.arange(0, d, 2, dtype=jnp.float32) / d)
            ang = jnp.outer(t, freqs)
            cos, sin = (jnp.cos(ang), jnp.sin(ang))
            xr = xh.reshape(xh.shape[:-1] + (d // 2, 2))
            x0, x1 = (xr[..., 0], xr[..., 1])
            rot = jnp.stack([x0 * cos - x1 * sin, x0 * sin + x1 * cos], axis=-1)
            return rot.reshape(xh.shape)

        def _attention(x, Wq, Wkva, Wkvb, Wo):
            b, t, _ = x.shape
            q = (x @ Wq).reshape(b, t, H, D).transpose(0, 2, 1, 3)
            ckv = x @ Wkva
            kv_latent, k_rope = (ckv[:, :, :R], ckv[:, :, R:])
            kv = (kv_latent @ Wkvb).reshape(b, t, H, NOPE).transpose(0, 2, 1, 3)
            k_rope = jnp.broadcast_to(k_rope[:, None, :, :], (b, H, t, ROPE))
            q_nope, q_rope = (q[..., :NOPE], q[..., NOPE:])
            q = jnp.concatenate([q_nope, _rope(q_rope)], axis=-1)
            k = jnp.concatenate([kv, _rope(k_rope)], axis=-1)
            v = jnp.concatenate([kv, jnp.zeros_like(k_rope)], axis=-1)
            att = jnp.einsum('bhqd,bhkd->bhqk', q, k) / jnp.sqrt(jnp.float32(D))
            mask = jnp.tril(jnp.ones((t, t), dtype=bool))
            att = jnp.where(mask, att, jnp.float32(-jnp.inf))
            att = jax.nn.softmax(att, axis=-1)
            y = jnp.einsum('bhqk,bhkd->bhqd', att, v)
            y = y.transpose(0, 2, 1, 3).reshape(b, t, H * D)
            return y @ Wo

        def _experts(x_flat, Wg, Wu, Wd):
            g = jax.nn.silu(jnp.einsum('nc,eci->nei', x_flat, Wg))
            u = jnp.einsum('nc,eci->nei', x_flat, Wu)
            return jnp.einsum('nei,eic->nec', g * u, Wd)

        def _moe(x, Wgate, expert_bias, Wg, Wu, Wd, sWg, sWu, sWd):
            b, t, c = x.shape
            xf = x.reshape(-1, c)
            shared = jnp.mean(_experts(xf, sWg, sWu, sWd), axis=1)
            logits = xf @ Wgate + expert_bias
            probs = jax.nn.softmax(logits, axis=-1)
            topk_p, topk_i = jax.lax.top_k(probs, K)
            topk_p = topk_p / jnp.sum(topk_p, axis=-1, keepdims=True)
            comb = jnp.sum(jax.nn.one_hot(topk_i, E, dtype=xf.dtype) * topk_p[..., None], axis=1)
            routed = jnp.einsum('ne,nec->nc', comb, _experts(xf, Wg, Wu, Wd))
            return (shared + routed).reshape(b, t, c)
        key = jax.random.key(seed)
        ks = jax.random.split(key, 16)
        w = lambda k, shp: jax.random.normal(k, shp, dtype=jnp.float32) * 0.02
        return {'x': jax.random.normal(ks[0], (B, T, C), dtype=jnp.float32), 'w_ln1': jnp.ones((C,), jnp.float32), 'Wq': w(ks[1], (C, H * D)), 'Wkva': w(ks[2], (C, R + ROPE)), 'Wkvb': w(ks[3], (R, H * NOPE)), 'Wo': w(ks[4], (H * D, C)), 'w_ln2': jnp.ones((C,), jnp.float32), 'Wgate': w(ks[5], (C, E)), 'expert_bias': jnp.zeros((E,), jnp.float32), 'Wg': w(ks[6], (E, C, I)), 'Wu': w(ks[7], (E, C, I)), 'Wd': w(ks[8], (E, I, C)), 'sWg': w(ks[9], (S, C, I)), 'sWu': w(ks[10], (S, C, I)), 'sWd': w(ks[11], (S, I, C))}
    _L0_ffn_all = _L0_ffn_setup()
    _L0_ffn_in = {k: v for k, v in _L0_ffn_all.items() if k in ('w_ln1', 'Wq', 'Wkva', 'Wkvb', 'Wo', 'w_ln2', 'Wgate', 'expert_bias', 'Wg', 'Wu', 'Wd', 'sWg', 'sWu', 'sWd')}
    del _L0_ffn_all

    def _L1_xattn_setup():
        import jax, jax.numpy as jnp
        import numpy as np
        DIM = 128
        NUM_HEADS = 16
        HEAD_DIM = DIM // NUM_HEADS
        key = jax.random.key(seed)
        ks = jax.random.split(key, 11)
        B, N, C = (2, 256, DIM)
        s = 1.0 / np.sqrt(C)
        inp = {'q': jax.random.normal(ks[0], (B, N, C), jnp.float32), 'k': jax.random.normal(ks[1], (B, N, C), jnp.float32), 'v': jax.random.normal(ks[2], (B, N, C), jnp.float32), 'Wq': jax.random.normal(ks[3], (C, C), jnp.float32) * s, 'bq': jnp.zeros((C,), jnp.float32), 'Wk': jax.random.normal(ks[4], (C, C), jnp.float32) * s, 'bk': jnp.zeros((C,), jnp.float32), 'Wv': jax.random.normal(ks[5], (C, C), jnp.float32) * s, 'bv': jnp.zeros((C,), jnp.float32), 'Wo': jax.random.normal(ks[6], (C, C), jnp.float32) * s, 'bo': jnp.zeros((C,), jnp.float32)}
        return inp
    _L1_xattn_all = _L1_xattn_setup()
    _L1_xattn_in = {k: v for k, v in _L1_xattn_all.items() if k in ('Wq', 'bq', 'Wk', 'bk', 'Wv', 'bv', 'Wo', 'bo')}
    del _L1_xattn_all

    def _L1_ffn_setup():
        import jax, jax.numpy as jnp
        import numpy as np
        B, T, D, F_FF, E, K = (8, 256, 128, 512, 8, 2)
        key = jax.random.key(seed)
        ks = jax.random.split(key, 6)
        s = 1.0 / np.sqrt(D)
        return {'x': jax.random.normal(ks[0], (B, T, D), jnp.float32), 'Wr': jax.random.normal(ks[1], (D, E), jnp.float32) * s, 'W1': jax.random.normal(ks[2], (E, D, F_FF), jnp.float32) * s, 'b1': jax.random.normal(ks[3], (E, F_FF), jnp.float32) * 0.01, 'W2': jax.random.normal(ks[4], (E, F_FF, D), jnp.float32) * (1.0 / np.sqrt(F_FF)), 'b2': jax.random.normal(ks[5], (E, D), jnp.float32) * 0.01}
    _L1_ffn_all = _L1_ffn_setup()
    _L1_ffn_in = {k: v for k, v in _L1_ffn_all.items() if k in ('Wr', 'W1', 'b1', 'W2', 'b2')}
    del _L1_ffn_all
    return {'x': x, 'ctx_1024': ctx_1024, 'mask_BxSxS2_if1': mask_BxSxS2_if1, 'g_xattn': g_xattn, 'g_ffn': g_ffn, 'L0_xattn_qw': _L0_xattn_in['qw'], 'L0_xattn_qb': _L0_xattn_in['qb'], 'L0_xattn_kw': _L0_xattn_in['kw'], 'L0_xattn_kb': _L0_xattn_in['kb'], 'L0_xattn_vw': _L0_xattn_in['vw'], 'L0_xattn_vb': _L0_xattn_in['vb'], 'L0_xattn_ow': _L0_xattn_in['ow'], 'L0_xattn_ob': _L0_xattn_in['ob'], 'L0_ffn_w_ln1': _L0_ffn_in['w_ln1'], 'L0_ffn_Wq': _L0_ffn_in['Wq'], 'L0_ffn_Wkva': _L0_ffn_in['Wkva'], 'L0_ffn_Wkvb': _L0_ffn_in['Wkvb'], 'L0_ffn_Wo': _L0_ffn_in['Wo'], 'L0_ffn_w_ln2': _L0_ffn_in['w_ln2'], 'L0_ffn_Wgate': _L0_ffn_in['Wgate'], 'L0_ffn_expert_bias': _L0_ffn_in['expert_bias'], 'L0_ffn_Wg': _L0_ffn_in['Wg'], 'L0_ffn_Wu': _L0_ffn_in['Wu'], 'L0_ffn_Wd': _L0_ffn_in['Wd'], 'L0_ffn_sWg': _L0_ffn_in['sWg'], 'L0_ffn_sWu': _L0_ffn_in['sWu'], 'L0_ffn_sWd': _L0_ffn_in['sWd'], 'L1_xattn_Wq': _L1_xattn_in['Wq'], 'L1_xattn_bq': _L1_xattn_in['bq'], 'L1_xattn_Wk': _L1_xattn_in['Wk'], 'L1_xattn_bk': _L1_xattn_in['bk'], 'L1_xattn_Wv': _L1_xattn_in['Wv'], 'L1_xattn_bv': _L1_xattn_in['bv'], 'L1_xattn_Wo': _L1_xattn_in['Wo'], 'L1_xattn_bo': _L1_xattn_in['bo'], 'L1_ffn_Wr': _L1_ffn_in['Wr'], 'L1_ffn_W1': _L1_ffn_in['W1'], 'L1_ffn_b1': _L1_ffn_in['b1'], 'L1_ffn_W2': _L1_ffn_in['W2'], 'L1_ffn_b2': _L1_ffn_in['b2']}

def reference(x, ctx_1024, mask_BxSxS2_if1, g_xattn, g_ffn, L0_xattn_qw, L0_xattn_qb, L0_xattn_kw, L0_xattn_kb, L0_xattn_vw, L0_xattn_vb, L0_xattn_ow, L0_xattn_ob, L0_ffn_w_ln1, L0_ffn_Wq, L0_ffn_Wkva, L0_ffn_Wkvb, L0_ffn_Wo, L0_ffn_w_ln2, L0_ffn_Wgate, L0_ffn_expert_bias, L0_ffn_Wg, L0_ffn_Wu, L0_ffn_Wd, L0_ffn_sWg, L0_ffn_sWu, L0_ffn_sWd, L1_xattn_Wq, L1_xattn_bq, L1_xattn_Wk, L1_xattn_bk, L1_xattn_Wv, L1_xattn_bv, L1_xattn_Wo, L1_xattn_bo, L1_ffn_Wr, L1_ffn_W1, L1_ffn_b1, L1_ffn_W2, L1_ffn_b2):
    import jax
    import jax.numpy as jnp

    def _L0_xattn_ref(query, key, value, mask, qw, qb, kw, kb, vw, vb, ow, ob):
        import jax, jax.numpy as jnp
        import numpy as np
        B, S, D, H = (2, 256, 128, 16)
        DH = D // H
        q = query @ qw.T + qb
        k = key @ kw.T + kb
        v = value @ vw.T + vb

        def split(x):
            b, s, _ = x.shape
            return x.reshape(b, s, H, DH).transpose(0, 2, 1, 3)
        qh, kh, vh = (split(q), split(k), split(v))
        scale = DH ** (-0.5)
        scores = jnp.einsum('bhqd,bhkd->bhqk', qh * scale, kh)
        scores = jnp.where(mask[:, None] == 0, jnp.float32(-1000000000.0), scores)
        probs = jax.nn.softmax(scores, axis=-1)
        out = jnp.einsum('bhqk,bhkd->bhqd', probs, vh)
        out = out.transpose(0, 2, 1, 3).reshape(out.shape[0], -1, H * DH)
        return out @ ow.T + ob

    def _L0_ffn_ref(x, w_ln1, Wq, Wkva, Wkvb, Wo, w_ln2, Wgate, expert_bias, Wg, Wu, Wd, sWg, sWu, sWd):
        import jax, jax.numpy as jnp
        import numpy as np
        B, T, C = (2, 256, 128)
        H, D = (16, 64)
        CR = 8
        R = C // CR
        ROPE = D // 2
        NOPE = D - ROPE
        E, K, I, S = (8, 2, 64, 1)
        THETA = 100000.0
        EPS = 1e-05

        def _rmsnorm(x, w):
            rms = jnp.sqrt(jnp.mean(x * x, axis=-1, keepdims=True) + EPS)
            return w * (x / rms)

        def _rope(xh):
            d = xh.shape[-1]
            t = jnp.arange(xh.shape[2], dtype=jnp.float32)
            freqs = 1.0 / THETA ** (jnp.arange(0, d, 2, dtype=jnp.float32) / d)
            ang = jnp.outer(t, freqs)
            cos, sin = (jnp.cos(ang), jnp.sin(ang))
            xr = xh.reshape(xh.shape[:-1] + (d // 2, 2))
            x0, x1 = (xr[..., 0], xr[..., 1])
            rot = jnp.stack([x0 * cos - x1 * sin, x0 * sin + x1 * cos], axis=-1)
            return rot.reshape(xh.shape)

        def _attention(x, Wq, Wkva, Wkvb, Wo):
            b, t, _ = x.shape
            q = (x @ Wq).reshape(b, t, H, D).transpose(0, 2, 1, 3)
            ckv = x @ Wkva
            kv_latent, k_rope = (ckv[:, :, :R], ckv[:, :, R:])
            kv = (kv_latent @ Wkvb).reshape(b, t, H, NOPE).transpose(0, 2, 1, 3)
            k_rope = jnp.broadcast_to(k_rope[:, None, :, :], (b, H, t, ROPE))
            q_nope, q_rope = (q[..., :NOPE], q[..., NOPE:])
            q = jnp.concatenate([q_nope, _rope(q_rope)], axis=-1)
            k = jnp.concatenate([kv, _rope(k_rope)], axis=-1)
            v = jnp.concatenate([kv, jnp.zeros_like(k_rope)], axis=-1)
            att = jnp.einsum('bhqd,bhkd->bhqk', q, k) / jnp.sqrt(jnp.float32(D))
            mask = jnp.tril(jnp.ones((t, t), dtype=bool))
            att = jnp.where(mask, att, jnp.float32(-jnp.inf))
            att = jax.nn.softmax(att, axis=-1)
            y = jnp.einsum('bhqk,bhkd->bhqd', att, v)
            y = y.transpose(0, 2, 1, 3).reshape(b, t, H * D)
            return y @ Wo

        def _experts(x_flat, Wg, Wu, Wd):
            g = jax.nn.silu(jnp.einsum('nc,eci->nei', x_flat, Wg))
            u = jnp.einsum('nc,eci->nei', x_flat, Wu)
            return jnp.einsum('nei,eic->nec', g * u, Wd)

        def _moe(x, Wgate, expert_bias, Wg, Wu, Wd, sWg, sWu, sWd):
            b, t, c = x.shape
            xf = x.reshape(-1, c)
            shared = jnp.mean(_experts(xf, sWg, sWu, sWd), axis=1)
            logits = xf @ Wgate + expert_bias
            probs = jax.nn.softmax(logits, axis=-1)
            topk_p, topk_i = jax.lax.top_k(probs, K)
            topk_p = topk_p / jnp.sum(topk_p, axis=-1, keepdims=True)
            comb = jnp.sum(jax.nn.one_hot(topk_i, E, dtype=xf.dtype) * topk_p[..., None], axis=1)
            routed = jnp.einsum('ne,nec->nc', comb, _experts(xf, Wg, Wu, Wd))
            return (shared + routed).reshape(b, t, c)
        x = x + _attention(_rmsnorm(x, w_ln1), Wq, Wkva, Wkvb, Wo)
        residual = x
        xn = _rmsnorm(x, w_ln2)
        x_out = _moe(xn, Wgate, expert_bias, Wg, Wu, Wd, sWg, sWu, sWd)
        return residual + x_out

    def _L1_xattn_ref(q, k, v, Wq, bq, Wk, bk, Wv, bv, Wo, bo):
        import jax, jax.numpy as jnp
        import numpy as np
        DIM = 128
        NUM_HEADS = 16
        HEAD_DIM = DIM // NUM_HEADS
        B, Nq, C = q.shape
        Nkv = k.shape[1]
        H, D = (NUM_HEADS, HEAD_DIM)
        qh = (q @ Wq.T + bq).reshape(B, Nq, H, D).transpose(0, 2, 1, 3)
        kh = (k @ Wk.T + bk).reshape(B, Nkv, H, D).transpose(0, 2, 1, 3)
        vh = (v @ Wv.T + bv).reshape(B, Nkv, H, D).transpose(0, 2, 1, 3)
        scale = D ** (-0.5)
        attn = jax.nn.softmax(jnp.einsum('bhqd,bhkd->bhqk', qh, kh) * scale, axis=-1)
        out = jnp.einsum('bhqk,bhkd->bhqd', attn, vh)
        out = out.transpose(0, 2, 1, 3).reshape(B, Nq, C)
        return out @ Wo.T + bo

    def _L1_ffn_ref(x, Wr, W1, b1, W2, b2):
        import jax, jax.numpy as jnp
        import numpy as np
        B, T, D, F_FF, E, K = (8, 256, 128, 512, 8, 2)
        pooled = x.mean(axis=1)
        logits = pooled @ Wr
        top_scores, top_idx = jax.lax.top_k(logits, K)
        weights = jax.nn.softmax(top_scores, axis=-1)
        W1s, b1s = (W1[top_idx], b1[top_idx])
        W2s, b2s = (W2[top_idx], b2[top_idx])
        h = jnp.einsum('btd,bkdf->bktf', x, W1s) + b1s[:, :, None, :]
        h = jax.nn.gelu(h, approximate=False)
        y = jnp.einsum('bktf,bkfd->bktd', h, W2s) + b2s[:, :, None, :]
        out = jnp.einsum('bk,bktd->btd', weights, y)
        return out
    x = x + jnp.tanh(g_xattn[0]) * _L0_xattn_ref(_layernorm(x, axis=-1), ctx_1024, ctx_1024, mask_BxSxS2_if1, L0_xattn_qw, L0_xattn_qb, L0_xattn_kw, L0_xattn_kb, L0_xattn_vw, L0_xattn_vb, L0_xattn_ow, L0_xattn_ob)
    x = x + jnp.tanh(g_ffn[0]) * _L0_ffn_ref(_layernorm(x, axis=-1), L0_ffn_w_ln1, L0_ffn_Wq, L0_ffn_Wkva, L0_ffn_Wkvb, L0_ffn_Wo, L0_ffn_w_ln2, L0_ffn_Wgate, L0_ffn_expert_bias, L0_ffn_Wg, L0_ffn_Wu, L0_ffn_Wd, L0_ffn_sWg, L0_ffn_sWu, L0_ffn_sWd)
    x = x + jnp.tanh(g_xattn[1]) * _L1_xattn_ref(_layernorm(x, axis=-1), ctx_1024, ctx_1024, L1_xattn_Wq, L1_xattn_bq, L1_xattn_Wk, L1_xattn_bk, L1_xattn_Wv, L1_xattn_bv, L1_xattn_Wo, L1_xattn_bo)
    x = x + jnp.tanh(g_ffn[1]) * _L1_ffn_ref(_layernorm(x, axis=-1), L1_ffn_Wr, L1_ffn_W1, L1_ffn_b1, L1_ffn_W2, L1_ffn_b2)
    return x

_drawn_inputs = setup_inputs


def setup_inputs(seed=0):
    import zlib

    import numpy as np

    out = dict(_drawn_inputs(seed))
    spreads = {'g_ffn': (-1.0, 0.6),
     'L0_xattn_qb': (0.0, 0.8),
     'L0_xattn_kb': (0.0, 2.0),
     'L0_xattn_vb': (0.0, 0.717),
     'L0_xattn_ob': (0.0, 0.1),
     'L0_ffn_w_ln1': (1.0, 0.6),
     'L0_ffn_w_ln2': (1.0, 0.6),
     'L0_ffn_expert_bias': (0.0, 0.8),
     'L1_xattn_bq': (0.0, 0.8),
     'L1_xattn_bk': (0.0, 2.0),
     'L1_xattn_bv': (0.0, 0.47),
     'L1_xattn_bo': (0.0, 0.403)}
    factors = {'L0_xattn_qw': 8.0,
     'L0_xattn_kw': 8.0,
     'L0_xattn_vw': 4.779,
     'L0_xattn_ow': 3.578,
     'L0_ffn_Wq': 8.0,
     'L0_ffn_Wkva': 8.0,
     'L0_ffn_Wkvb': 8.0,
     'L0_ffn_Wo': 8.0,
     'L0_ffn_Wgate': 8.0,
     'L0_ffn_Wg': 8.0,
     'L0_ffn_Wu': 8.0,
     'L0_ffn_Wd': 8.0,
     'L0_ffn_sWg': 6.264,
     'L0_ffn_sWu': 6.146,
     'L0_ffn_sWd': 6.304,
     'L1_ffn_b1': 64.0,
     'L1_ffn_b2': 52.376}
    for name, (base, spread) in spreads.items():
        noise = np.random.default_rng([zlib.crc32(name.encode()), seed]).standard_normal(out[name].shape)
        drawn = base * np.exp(spread * noise) if base else spread * noise
        out[name] = jnp.asarray(drawn.astype(out[name].dtype))
    for name, factor in factors.items():
        out[name] = (out[name] * factor).astype(out[name].dtype)
    return out
```

```python
from contextlib import ExitStack

import numpy as np

import concourse.bass as bass
from concourse import mybir

F32 = mybir.dt.float32
I32 = mybir.dt.int32
U32 = mybir.dt.uint32
BF16 = mybir.dt.bfloat16
ALU = mybir.AluOpType
ACT = mybir.ActivationFunctionType
AX = mybir.AxisListType

C = 128
T = 56
KEYS = 1500
H = 16
DH = C // H
PAIRS = H // 2
ROWS = 2 * T
KC = 125
KCH = KEYS // KC
SB = 3
SW = KEYS // SB
TB = KCH // SB
VB = 3
VJ = KCH // VB
MASKED = -1.0e9
Q_PART = (0, 0, 1, 1, 0, 2)
K_PART = (0, 1, 0, 1, 2, 0)
SLOTS = len(Q_PART)
KEY_ORDER = np.arange(C).reshape(PAIRS, 2 * DH).T.reshape(C)
EPS = 1e-5

HF = 16
NOPE = 32
ROPE = 32
RANK = 16
KD = RANK + ROPE
THETA = 100000.0
E = 8
I0 = 64
F1 = 512
FB = F1 // C


def chunks_of(tokens):
    w = 8 * T if tokens % (8 * T) == 0 else 2 * T
    return w, tokens // w


def phase_semaphores(nc, ctx, ph):
    mine = []

    def sem(name):
        mine.append(nc.alloc_semaphore(ph + name))
        return mine[-1]

    def close():
        nc.clear_and_free_semaphores(mine)
        nc.all_engine_barrier()

    ctx.callback(close)
    return sem


def norm_phase(nc, res, src_gate, want_rms, ph):
    XT, XN, UPD = res["XT"], res["XN"], res["UPD"]
    tokens = res["tokens"]
    W, N = chunks_of(tokens)
    with ExitStack() as ctx:
        sem = phase_semaphores(nc, ctx, ph)
        sb = lambda n, s: ctx.enter_context(nc.sbuf_tensor(ph + n, s, F32))
        dev = sb("dev", [C, 2, W])
        sq = sb("sq", [C, 2, W])
        sd = sb("sd", [C, 2, W])
        mean_ps = [ctx.enter_context(nc.psum_tensor(ph + f"mean{i}", [C, 512], F32)) for i in range(2)]
        var_ps = [ctx.enter_context(nc.psum_tensor(ph + f"var{i}", [C, 512], F32)) for i in range(2)]
        ms_ps = [ctx.enter_context(nc.psum_tensor(ph + f"ms{i}", [C, 512], F32)) for i in range(2)]
        x_ready = sem("x_ready")
        mean_done = sem("mean_done")
        dev_ready = sem("dev_ready")
        sq_ready = sem("sq_ready")
        var_done = sem("var_done")
        sd_ready = sem("sd_ready")
        rstd_ready = sem("rstd_ready")
        xn_ready = sem("xn_ready")
        sq2_ready = sem("sq2_ready")
        ms_done = sem("ms_done")
        sd2_ready = sem("sd2_ready")
        rrms_ready = sem("rrms_ready")
        h_ready = sem("h_ready")
        block = ctx.enter_context(nc.Block())

        def cols(n):
            return slice(n * W, n * W + W)

        @block.tensor
        def _(pe):
            for n in range(N):
                if src_gate is not None:
                    pe.wait_ge(x_ready, n + 1)
                if n >= 2:
                    pe.wait_ge(dev_ready, n - 1)
                pe.matmul(mean_ps[n % 2][:, 0:W], res["avg"][:, :], XT[:, cols(n)], start=True, stop=True).then_inc(mean_done, 1)
                pe.wait_ge(sq_ready, n + 1)
                if n >= 2:
                    pe.wait_ge(sd_ready, n - 1)
                pe.matmul(var_ps[n % 2][:, 0:W], res["avg"][:, :], sq[:, n % 2, :], start=True, stop=True).then_inc(var_done, 1)
                if want_rms is not None:
                    pe.wait_ge(sq2_ready, n + 1)
                    if n >= 2:
                        pe.wait_ge(sd2_ready, n - 1)
                    pe.matmul(ms_ps[n % 2][:, 0:W], res["avg"][:, :], sq[:, n % 2, :], start=True, stop=True).then_inc(ms_done, 1)

        @block.scalar
        def _(act):
            for n in range(N):
                act.wait_ge(dev_ready, n + 1)
                if n >= 2:
                    act.wait_ge(ms_done if want_rms is not None else var_done, n - 1)
                act.activation(sq[:, n % 2, :], dev[:, n % 2, :], ACT.Square).then_inc(sq_ready, 1)
                act.wait_ge(var_done, n + 1)
                if n >= 2:
                    act.wait_ge(rrms_ready if want_rms is not None else rstd_ready, n - 1)
                act.activation(sd[:, n % 2, :], var_ps[n % 2][:, 0:W], ACT.Sqrt, bias=res["eps"][:, 0:1]).then_inc(sd_ready, 1)
                if want_rms is not None:
                    act.wait_ge(xn_ready, n + 1)
                    act.activation(sq[:, n % 2, :], XN[:, cols(n)], ACT.Square).then_inc(sq2_ready, 1)
                    act.wait_ge(ms_done, n + 1)
                    act.activation(sd[:, n % 2, :], ms_ps[n % 2][:, 0:W], ACT.Sqrt, bias=res["eps"][:, 0:1]).then_inc(sd2_ready, 1)

        @block.vector
        def _(dve):
            for n in range(N):
                if src_gate is not None:
                    dve.scalar_tensor_tensor(XT[:, cols(n)], UPD[:, cols(n)], src_gate, XT[:, cols(n)], ALU.mult, ALU.add).then_inc(x_ready, 1)
                    dve.wait_ge(x_ready, n + 1)
                dve.wait_ge(mean_done, n + 1)
                if n >= 2:
                    dve.wait_ge(sq_ready, n - 1)
                dve.tensor_tensor(dev[:, n % 2, :], XT[:, cols(n)], mean_ps[n % 2][:, 0:W], ALU.subtract).then_inc(dev_ready, 1)
                dve.wait_ge(sd_ready, n + 1)
                dve.reciprocal(sd[:, n % 2, :], sd[:, n % 2, :]).then_inc(rstd_ready, 1)
                dve.wait_ge(rstd_ready, n + 1)
                dve.tensor_tensor(XN[:, cols(n)], dev[:, n % 2, :], sd[:, n % 2, :], ALU.mult).then_inc(xn_ready, 1)
                if want_rms is not None:
                    w, out = want_rms
                    dve.wait_ge(sd2_ready, n + 1)
                    dve.reciprocal(sd[:, n % 2, :], sd[:, n % 2, :]).then_inc(rrms_ready, 1)
                    dve.wait_ge(rrms_ready, n + 1)
                    dve.scalar_tensor_tensor(out[:, cols(n)], XN[:, cols(n)], w, sd[:, n % 2, :], ALU.mult, ALU.mult).then_inc(h_ready, 1)


def load_phase(nc, res, ins, ph):
    with ExitStack() as ctx:
        sem = phase_semaphores(nc, ctx, ph)
        loaded = sem("loaded")
        made = sem("made")
        qsel32 = ctx.enter_context(nc.sbuf_tensor(ph + "qsel32", res["qsel"].shape, F32))
        block = ctx.enter_context(nc.Block())
        todo = [(res["XT"], ins["xT"]), (res["gates"], ins["gates"]), (res["ident"], ins["ident"]),
                (res["slothead"], ins["slothead"]), (res["rowsel"], ins["rowsel"]), (res["groupsum"], ins["groupsum"]), (res["rmsw"], ins["rmsw"])]

        @block.sync
        def _(sp):
            for dst, src in todo:
                sp.dma_start(dst[:, :], src).then_inc(loaded, 16)
            sp.dma_start(qsel32[:, :, :, :], ins["qsel"]).then_inc(loaded, 16)
            sp.wait_ge(loaded, 16 * (len(todo) + 1))

        @block.vector
        def _(dve):
            dve.memset(res["avg"][:, :], 1.0 / C).then_inc(made, 1)
            dve.memset(res["eps"][:, :], EPS).then_inc(made, 1)
            dve.wait_ge(loaded, 16 * (len(todo) + 1))
            dve.tensor_copy(res["qsel"][:, :, :, :], qsel32[:, :, :, :]).then_inc(made, 1)

        @block.scalar
        def _(act):
            act.wait_ge(loaded, 16 * (len(todo) + 1))
            act.activation(res["gates"][:, :], res["gates"][:, :], ACT.Tanh).then_inc(made, 1)


def xattn_phase(nc, res, w, mask, ph):
    XN, UPD, B = res["XN"], res["UPD"], res["B"]
    tokens = res["tokens"]
    masked = mask is not None
    W, N = chunks_of(tokens)
    with ExitStack() as ctx:
        sem = phase_semaphores(nc, ctx, ph)
        sb = lambda n, s, d=F32: ctx.enter_context(nc.sbuf_tensor(ph + n, s, d))
        pb = lambda n, s: ctx.enter_context(nc.psum_tensor(ph + n, s, F32))
        q32 = sb("q32", [C, tokens])
        qpart = sb("qpart", [C, 3, tokens], BF16)
        wq = sb("wq", [C, C])
        wk = sb("wk", [C, C])
        wv = sb("wv", [C, C])
        wo = sb("wo", [C, C])
        bias = sb("bias", [C, 3])
        vbias = sb("vbias", [C, C])
        ctxT = sb("ctxT", [C, 2, KEYS])
        kpart = sb("kpart", [C, 3, KEYS], BF16)
        krest = sb("krest", [C, 2, SW])
        kpack = sb("kpack", [SLOTS * 2 * DH, 2, PAIRS, KEYS], BF16)
        qpack = sb("qpack", [SLOTS * 2 * DH, 2, PAIRS, 2, T], BF16)
        vx = sb("vx", [KC, 2, KCH, PAIRS, 32])
        maskb = sb("maskb", [ROWS, 2, KEYS], I32 if masked else F32) if masked else None
        s_sb = sb("s_sb", [ROWS, 2, KEYS])
        p_sb = sb("p_sb", [ROWS, 2, KEYS])
        pT = sb("pT", [KC, 2, KCH * ROWS])
        mx = sb("mx", [ROWS, 4])
        live = sb("live", [ROWS, 4])
        nb = sb("nb", [ROWS, 4])
        carrier = sb("carrier", [ROWS, 1])
        pool_carrier = sb("pool_carrier", [C, 1])
        zero = sb("zero", [C, 1])
        rowsum = sb("rowsum", [ROWS, 2, PAIRS])
        rrow = sb("rrow", [ROWS, PAIRS])
        pv_sb = sb("pv_sb", [C, 2, 4 * ROWS])
        o_sel = sb("o_sel", [ROWS, PAIRS, 2 * DH])
        o_nrm = sb("o_nrm", [ROWS, PAIRS, 2 * DH])
        oT = sb("oT", [C, ROWS])
        score_ps = pb("score_ps", [C, SB, 512])
        pT_ps = pb("pT_ps", [C, SB, 512])
        pv_ps = pb("pv_ps", [C, 512])
        misc_ps = pb("misc_ps", [C, 512])

        w_dma = sem("w_dma")
        vx_zero = sem("vx_zero")
        q_done = sem("q_done")
        q32_ready = sem("q32_ready")
        q0_ready = sem("q0_ready")
        qrest_ready = sem("qrest_ready")
        q1_ready = sem("q1_ready")
        q2_ready = sem("q2_ready")
        ctx_dma = [sem("ctx_dma0"), sem("ctx_dma1")]
        mask_dma = [sem("mask_dma0"), sem("mask_dma1")]
        mask_ready = sem("mask_ready")
        qpack_done = sem("qpack_done")
        qpack_ready = sem("qpack_ready")
        k0_ready = sem("k0_ready")
        k1_ready = sem("k1_ready")
        k2_ready = sem("k2_ready")
        kpack_dma = [sem("kpack_dma0"), sem("kpack_dma1")]
        kv_done = sem("kv_done")
        kv_ready = sem("kv_ready")
        s_done = sem("s_done")
        s_taken = sem("s_taken")
        live_ready = sem("live_ready")
        nb_ready = sem("nb_ready")
        p_ready = sem("p_ready")
        pT_done = sem("pT_done")
        pT_ready = sem("pT_ready")
        pv_done = sem("pv_done")
        pv_taken = sem("pv_taken")
        sel_done = sem("sel_done")
        recip_ready = sem("recip_ready")
        osel_ready = sem("osel_ready")
        onrm_ready = sem("onrm_ready")
        oT_done = sem("oT_done")
        oT_ready = sem("oT_ready")
        out_done = sem("out_done")
        out_taken = sem("out_taken")
        block = ctx.enter_context(nc.Block())

        def over_batches(eng, batch):
            pairs = B // 2

            def pair(i, first, last):
                batch(i, 0, first, False)
                batch(i, 1, False, last)

            pair(0, True, pairs == 1)
            if pairs > 2:
                with eng.Fori(1, pairs - 1) as i:
                    pair(i, False, False)
            if pairs > 1:
                pair(pairs - 1, False, True)

        def early(i):
            return isinstance(i, int) and i == 0

        @block.sync
        def _(sp):
            for dst, src in ((wq, w["qwT"]), (wk, w["kwT"]), (wv, w["vwT"]), (wo, w["owT"]), (bias, w["bias"]), (vbias, w["vb"])):
                sp.dma_start(dst[:, :], src).then_inc(w_dma, 16)

            def load_context(i, s):
                b = 2 * i + s
                if not early(i):
                    sp.wait_ge(kv_done, 6 * (b - 1))
                sp.dma_start(ctxT[:, s, :], w["ctxT"][bass.ds(b, 1), :, :].rearrange("a c k -> (a c) k")).then_inc(ctx_dma[s], 16)

            def load_mask(i, s):
                b = 2 * i + s
                if masked:
                    if not early(i):
                        sp.wait_ge(s_taken, PAIRS * (b - 1))
                    for half in range(2):
                        sp.dma_start(maskb[half * T:half * T + T, s, :], mask[bass.ds(b, 1), :, :].rearrange("a q k -> (a q) k")).then_inc(mask_dma[s], 16)

            def pack_keys(i, s):
                b = 2 * i + s
                sp.wait_ge(k2_ready, SB * b + SB)
                for slot, part in enumerate(K_PART):
                    sp.dma_start(kpack[slot * 2 * DH:(slot + 1) * 2 * DH, s, :, :], kpart[:, part, :]).then_inc(kpack_dma[s], 16)

            for s in range(2):
                load_context(0, s)
                load_mask(0, s)
            pack_keys(0, 0)

            def ahead(i):
                load_context(i + 1, 0)
                pack_keys(i, 1)
                load_mask(i + 1, 0)
                load_context(i + 1, 1)
                pack_keys(i + 1, 0)
                load_mask(i + 1, 1)

            if B > 2:
                ahead(0)
            if B > 4:
                with sp.Fori(1, B // 2 - 1) as i:
                    ahead(i)
            pack_keys(B // 2 - 1, 1)

        @block.gpsimd
        def _(pool):
            pool.memset(vx[:, :, :, :, 2 * DH:32], 0.0).then_inc(vx_zero, 1)
            pool.memset(zero[:, :], 0.0).then_inc(vx_zero, 1)
            pool.wait_ge(vx_zero, 2)

            def split_keys(b):
                for u in range(SB):
                    cols = slice(u * SW, (u + 1) * SW)
                    pool.wait_ge(kv_ready, 6 * b + u + 1)
                    pool.tensor_tensor(kpart[:, 1, cols], krest[:, u % 2, :], zero[:, 0:1].to_broadcast([C, SW]), ALU.add).then_inc(k1_ready, 1)
                    pool.wait_ge(k1_ready, SB * b + u + 1)
                    pool.tensor_tensor(kpart[:, 2, cols], krest[:, u % 2, :], kpart[:, 1, cols], ALU.subtract).then_inc(k2_ready, 1)

            def make_mask(i, s):
                if masked:
                    pool.wait_ge(mask_dma[s], 32 * (i + 1))
                    if not (early(i) and s == 0):
                        pool.wait_ge(mask_ready, 2 * i + s)
                    pool.tensor_tensor(pool_carrier[:, :], res["eps"][:, :], res["eps"][:, :], ALU.add)
                    pool.tensor_scalar(maskb[:, s, :].bitcast(F32), maskb[:, s, :], 0.0, MASKED, ALU.is_equal, ALU.mult).then_inc(mask_ready, 1)

            def batch(i, s, first, last):
                if not last:
                    split_keys(2 * i + s + 1)
                if not last and not (early(i) and s == 0):
                    make_mask(i + s, 1 - s)

            split_keys(0)
            make_mask(0, 0)
            make_mask(0, 1)
            over_batches(pool, batch)

        @block.tensor
        def _(pe):
            def kv_unit(b, s, u):
                if u < SB:
                    mm = pe.matmul(misc_ps[:, 0:SW], wk[:, :], ctxT[:, s, u * SW:(u + 1) * SW], start=True, stop=True)
                else:
                    for jj in range(VJ):
                        j = (u - SB) * VJ + jj
                        mm = pe.matmul(misc_ps[0:KC, jj * C:(jj + 1) * C], ctxT[:, s, j * KC:(j + 1) * KC], wv[:, :], start=True, stop=True)
                mm.then_inc(kv_done, 1)

            def place_queries(b):
                for p in range(PAIRS):
                    for part in range(3):
                        mm = pe.matmul(misc_ps[0:SLOTS * 2 * DH, p * T:(p + 1) * T], res["qsel"][:, part, p, :], qpart[:, part, bass.ds(b * T, T)], start=(part == 0), stop=(part == 2))
                mm.then_inc(qpack_done, 1)

            def scores(i, s, t, first):
                b = 2 * i + s
                if t == 0:
                    pe.wait_ge(qpack_ready, 2 * b + 2)
                    pe.wait_ge(kpack_dma[s], 16 * SLOTS * (i + 1))
                if not (first and t == 0):
                    pe.wait_ge(s_taken, PAIRS * b + t)
                for k in range(SB):
                    mm = pe.matmul(score_ps[0:ROWS, k, 0:SW], qpack[:, s, t, :, :].rearrange("x h q -> x (h q)"), kpack[:, s, t, k * SW:(k + 1) * SW], start=True, stop=True)
                mm.then_inc(s_done, 1)

            def transposes(b, t, first):
                n = PAIRS * b + t
                pe.wait_ge(p_ready, n + 1)
                if not (first and t == 0):
                    pe.wait_ge(pT_ready, n)
                for j in range(KCH):
                    mm = pe.transpose(pT_ps[0:KC, j // TB, (j % TB) * ROWS:(j % TB + 1) * ROWS], p_sb[:, t % 2, j * KC:(j + 1) * KC], res["ident"][0:ROWS, 0:ROWS])
                mm.then_inc(pT_done, 1)

            def values(b, s, t, first):
                pe.wait_ge(pT_ready, PAIRS * b + t + 1)
                if t == 0 and not first:
                    pe.wait_ge(pv_taken, 2 * b)
                if t == 4:
                    pe.wait_ge(pv_taken, 2 * b + 1)
                for j in range(KCH):
                    g = j % 4
                    mm = pe.matmul(pv_ps[32 * g:32 * g + 32, (t % 4) * ROWS:(t % 4 + 1) * ROWS], vx[:, s, j, t, :], pT[:, t % 2, j * ROWS:(j + 1) * ROWS], start=(j < 4), stop=(j >= KCH - 4))
                mm.then_inc(pv_done, 1)

            def select(b):
                pe.wait_ge(pv_taken, 2 * b + 2)
                for t in range(PAIRS):
                    mm = pe.matmul(misc_ps[0:ROWS, t * 2 * DH:(t + 1) * 2 * DH], pv_sb[:, t // 4, (t % 4) * ROWS:(t % 4 + 1) * ROWS], res["groupsum"][:, :], start=True, stop=True)
                mm.then_inc(sel_done, 1)

            def turn(b):
                pe.wait_ge(onrm_ready, b + 1)
                pe.transpose(misc_ps[:, 0:ROWS], o_nrm[:, :, :].rearrange("r p d -> r (p d)"), res["ident"][0:ROWS, 0:ROWS]).then_inc(oT_done, 1)

            def project(b):
                pe.wait_ge(oT_ready, b + 1)
                pe.matmul(misc_ps[:, 0:T], wo[:, :], oT[:, 0:T], start=True, stop=False)
                pe.matmul(misc_ps[:, 0:T], wo[:, :], oT[:, T:ROWS], start=False, stop=True).then_inc(out_done, 1)

            def batch(i, s, first, last):
                b = 2 * i + s
                for t in range(PAIRS):
                    scores(i, s, t, first)
                    if not last and t < 2 * SB:
                        if t == 0:
                            pe.wait_ge(ctx_dma[1 - s], 16 * (i + 1 + s))
                            pe.wait_ge(qpack_ready, 2 * b + 2)
                        else:
                            pe.wait_ge(kv_ready, 6 * b + 6 + t)
                        if not first and t == 4:
                            pe.wait_ge(osel_ready, b)
                        if not first and t == 5:
                            pe.wait_ge(oT_ready, b)
                        kv_unit(b + 1, 1 - s, t)
                    if not last and t == 2 * SB:
                        pe.wait_ge(kv_ready, 6 * b + 12)
                        if not first:
                            pe.wait_ge(out_taken, b)
                        place_queries(b + 1)
                    if t >= 2:
                        transposes(b, t - 2, first)
                    elif not first:
                        transposes(b - 1, t + PAIRS - 2, False)
                    if t >= 3:
                        values(b, s, t - 3, first)
                    elif not first:
                        values(b - 1, 1 - s, t + PAIRS - 3, False)
                    if not first and 3 <= t <= 5:
                        if not last:
                            pe.wait_ge(kv_ready, 6 * b + 6 + t + 1)
                        if t == 3:
                            select(b - 1)
                        elif t == 4:
                            turn(b - 1)
                        else:
                            project(b - 1)

            pe.wait_ge(w_dma, 16 * 6)
            for n in range(N):
                if n >= 1:
                    pe.wait_ge(q32_ready, n)
                pe.matmul(misc_ps[:, 0:W], wq[:, :], XN[:, n * W:(n + 1) * W], start=True, stop=True).then_inc(q_done, 1)
            pe.wait_ge(q32_ready, N)
            pe.wait_ge(ctx_dma[0], 16)
            for u in range(2 * SB):
                if u:
                    pe.wait_ge(kv_ready, u)
                kv_unit(0, 0, u)
            pe.wait_ge(kv_ready, 2 * SB)
            pe.wait_ge(q2_ready, N)
            place_queries(0)
            over_batches(pe, batch)
            b = B - 1
            for t in (PAIRS - 2, PAIRS - 1):
                transposes(b, t, False)
                values(b, 1, t - 1, False)
            values(b, 1, PAIRS - 1, False)
            pe.wait_ge(out_taken, b)
            select(b)
            turn(b)
            project(b)

        @block.scalar
        def _(act):
            def exps(b, s, t, first):
                n = PAIRS * b + t
                act.wait_ge(nb_ready, n + 1)
                if not (first and t < 2):
                    act.wait_ge(pT_done, n - 1)
                if t == 0 and not early_b[0]:
                    act.wait_ge(osel_ready, b - 1)
                act.activation(p_sb[:, t % 2, :], s_sb[:, t % 2, :], ACT.Exp, bias=nb[:, t % 4:t % 4 + 1],
                               scale=live[:, t % 4:t % 4 + 1] if masked else 1.0, accum_out=rowsum[:, s, t:t + 1]).then_inc(p_ready, 1)

            def evacuate(b, t, first):
                n = PAIRS * b + t
                act.wait_ge(pT_done, n + 1)
                if not (first and t < 2):
                    act.wait_ge(pv_done, n - 1)
                act.activation(pT[:, t % 2, :].rearrange("p (k w) -> p k w", k=SB), pT_ps[0:KC, :, 0:TB * ROWS], ACT.Copy).then_inc(pT_ready, 1)

            def first_part(b, u, packed):
                act.wait_ge(kv_done, 6 * b + u + 1)
                if u == 0 and packed is not None:
                    act.wait_ge(kpack_dma[packed[0]], packed[1])
                act.activation(kpart[:, 0, u * SW:(u + 1) * SW], misc_ps[:, 0:SW], ACT.Identity, bias=bias[:, 1:2]).then_inc(k0_ready, 1)

            def take_queries(b, s):
                act.wait_ge(qpack_done, b + 1)
                for hh in range(2):
                    act.activation(qpack[:, s, :, hh, :], misc_ps[0:SLOTS * 2 * DH, 0:PAIRS * T].rearrange("x (p q) -> x p q", q=T), ACT.Copy, scale=res["slothead"][:, hh:hh + 1]).then_inc(qpack_ready, 1)

            early_b = [False]

            def batch(i, s, first, last):
                b = 2 * i + s
                early_b[0] = early(i)
                for t in range(PAIRS):
                    if not last and t < SB:
                        first_part(b + 1, t, (s, 16 * SLOTS * (i + 1)))
                    if not last and t == 2 * SB:
                        take_queries(b + 1, 1 - s)
                    if t >= 2:
                        evacuate(b, t - 2, first)
                    elif not first:
                        evacuate(b - 1, t + PAIRS - 2, False)
                    exps(b, s, t, first)

            for n in range(N):
                cols = slice(n * W, (n + 1) * W)
                act.wait_ge(q32_ready, n + 1)
                act.activation(qpart[:, 0, cols], q32[:, cols], ACT.Copy).then_inc(q0_ready, 1)
                act.wait_ge(qrest_ready, n + 1)
                act.activation(qpart[:, 1, cols], q32[:, cols], ACT.Copy).then_inc(q1_ready, 1)
            for u in range(SB):
                first_part(0, u, None)
            take_queries(0, 0)
            over_batches(act, batch)
            for t in (PAIRS - 2, PAIRS - 1):
                evacuate(B - 1, t, False)

        @block.vector
        def _(dve):
            def take_scores(b, s, t, first):
                n = PAIRS * b + t
                col = slice(t % 4, t % 4 + 1)
                dve.wait_ge(s_done, n + 1)
                if not (first and t < 2):
                    dve.wait_ge(p_ready, n - 1)
                out3 = s_sb[:, t % 2, :].rearrange("r (k w) -> r k w", k=SB)
                if masked:
                    if t == 0:
                        dve.wait_ge(mask_ready, b + 1)
                    dve.memset(carrier[:, :], 0.0)
                    m3 = maskb[:, s, :].bitcast(F32).rearrange("r (k w) -> r k w", k=SB)
                    dve.tensor_tensor_reduce(out3, score_ps[0:ROWS, :, 0:SW], m3, 1.0, -3.0e38, ALU.add, ALU.max, mx[:, col]).then_inc(s_taken, 1)
                    dve.wait_ge(s_taken, n + 1)
                    dve.tensor_scalar(live[:, col], mx[:, col], MASKED / 2, None, ALU.is_gt).then_inc(live_ready, 1)
                    dve.wait_ge(live_ready, n + 1)
                    dve.scalar_tensor_tensor(nb[:, col], mx[:, col], -1.0, live[:, col], ALU.mult, ALU.mult).then_inc(nb_ready, 1)
                else:
                    dve.tensor_scalar(out3, score_ps[0:ROWS, :, 0:SW], 1.0, None, ALU.mult, ALU.max, accum_out=mx[:, col]).then_inc(s_taken, 1)
                    dve.wait_ge(s_taken, n + 1)
                    dve.tensor_scalar(nb[:, col], mx[:, col], -1.0, None, ALU.mult).then_inc(nb_ready, 1)

            def take_kv(b, s, u):
                dve.wait_ge(kv_done, 6 * b + u + 1)
                if u < SB:
                    dve.wait_ge(k0_ready, SB * b + u + 1)
                    if u == 2 or not (isinstance(b, int) and b == 0):
                        dve.wait_ge(k2_ready, SB * b + u - 1)
                    dve.scalar_tensor_tensor(krest[:, u % 2, :], misc_ps[:, 0:SW], bias[:, 1:2], kpart[:, 0, u * SW:(u + 1) * SW], ALU.add, ALU.subtract).then_inc(kv_ready, 1)
                else:
                    j = (u - SB) * VJ
                    vb = vbias[0:KC, :].rearrange("k (p d) -> k p d", d=2 * DH)
                    for jj in range(VJ):
                        ins = dve.tensor_tensor(vx[:, s, j + jj, :, 0:2 * DH], misc_ps[0:KC, jj * C:(jj + 1) * C].rearrange("k (p d) -> k p d", d=2 * DH), vb, ALU.add)
                    ins.then_inc(kv_ready, 1)

            def take_pv(b, half):
                dve.wait_ge(pv_done, PAIRS * b + 4 * half + 4)
                dve.tensor_copy(pv_sb[:, half, :], pv_ps[:, 0:4 * ROWS]).then_inc(pv_taken, 1)

            def normalise(b, s):
                dve.wait_ge(p_ready, PAIRS * (b + 1))
                dve.reciprocal(rrow[:, :], rowsum[:, s, :]).then_inc(recip_ready, 1)
                dve.wait_ge(sel_done, b + 1)
                own = res["rowsel"][0:ROWS, :].unsqueeze(1).to_broadcast([ROWS, PAIRS, 2 * DH])
                dve.tensor_tensor(o_sel[:, :, :], misc_ps[0:ROWS, 0:C].rearrange("r (p d) -> r p d", d=2 * DH), own, ALU.mult).then_inc(osel_ready, 1)
                dve.wait_ge(recip_ready, b + 1)
                dve.wait_ge(osel_ready, b + 1)
                dve.tensor_tensor(o_nrm[:, :, :], o_sel[:, :, :], rrow[:, :].unsqueeze(2).to_broadcast([ROWS, PAIRS, 2 * DH]), ALU.mult).then_inc(onrm_ready, 1)

            def take_turned(b):
                dve.wait_ge(oT_done, b + 1)
                dve.tensor_copy(oT[:, :], misc_ps[:, 0:ROWS]).then_inc(oT_ready, 1)

            def take_out(b):
                dve.wait_ge(out_done, b + 1)
                dve.tensor_scalar(UPD[:, bass.ds(b * T, T)], misc_ps[:, 0:T], bias[:, 2:3], None, ALU.add).then_inc(out_taken, 1)

            def batch(i, s, first, last):
                b = 2 * i + s
                for t in range(PAIRS):
                    take_scores(b, s, t, first)
                    if not last and t < 2 * SB:
                        take_kv(b + 1, 1 - s, t)
                    if not first:
                        if t == 2:
                            take_pv(b - 1, 1)
                        elif t == 3:
                            normalise(b - 1, 1 - s)
                        elif t == 4:
                            take_turned(b - 1)
                        elif t == 5:
                            take_out(b - 1)
                    if t == 6:
                        take_pv(b, 0)

            dve.wait_ge(w_dma, 16 * 6)
            for n in range(N):
                dve.wait_ge(q_done, n + 1)
                cols = slice(n * W, (n + 1) * W)
                dve.tensor_scalar(q32[:, cols], misc_ps[:, 0:W], bias[:, 0:1], float(DH) ** -0.5, ALU.add, ALU.mult).then_inc(q32_ready, 1)
                dve.wait_ge(q0_ready, n + 1)
                dve.tensor_tensor(q32[:, cols], q32[:, cols], qpart[:, 0, cols], ALU.subtract).then_inc(qrest_ready, 1)
                dve.wait_ge(qrest_ready, n + 1)
                dve.wait_ge(q1_ready, n + 1)
                dve.tensor_tensor(qpart[:, 2, cols], q32[:, cols], qpart[:, 1, cols], ALU.subtract).then_inc(q2_ready, 1)
            dve.wait_ge(vx_zero, 2)
            for u in range(2 * SB):
                take_kv(0, 0, u)
            over_batches(dve, batch)
            take_pv(B - 1, 1)
            normalise(B - 1, 1)
            take_turned(B - 1)
            take_out(B - 1)


def rms_phase(nc, res, src, dst, w, ph):
    W, N = chunks_of(res["tokens"])
    with ExitStack() as ctx:
        sem = phase_semaphores(nc, ctx, ph)
        sq = ctx.enter_context(nc.sbuf_tensor(ph + "sq", [C, N, W], F32))
        sd = ctx.enter_context(nc.sbuf_tensor(ph + "sd", [C, N, W], F32))
        ms_ps = ctx.enter_context(nc.psum_tensor(ph + "ms", [C, N, 512], F32))
        sq_ready = sem("sq_ready")
        ms_done = sem("ms_done")
        sd_ready = sem("sd_ready")
        rrms_ready = sem("rrms_ready")
        dst_ready = sem("dst_ready")
        block = ctx.enter_context(nc.Block())

        @block.tensor
        def _(pe):
            for n in range(N):
                pe.wait_ge(sq_ready, n + 1)
                pe.matmul(ms_ps[:, n, 0:W], res["avg"][:, :], sq[:, n, :], start=True, stop=True).then_inc(ms_done, 1)

        @block.scalar
        def _(act):
            for n in range(N):
                act.activation(sq[:, n, :], src[:, n * W:(n + 1) * W], ACT.Square).then_inc(sq_ready, 1)
            for n in range(N):
                act.wait_ge(ms_done, n + 1)
                act.activation(sd[:, n, :], ms_ps[:, n, 0:W], ACT.Sqrt, bias=res["eps"][:, 0:1]).then_inc(sd_ready, 1)

        @block.vector
        def _(dve):
            for n in range(N):
                dve.wait_ge(sd_ready, n + 1)
                dve.reciprocal(sd[:, n, :], sd[:, n, :]).then_inc(rrms_ready, 1)
                dve.wait_ge(rrms_ready, n + 1)
                dve.scalar_tensor_tensor(dst[:, n * W:(n + 1) * W], src[:, n * W:(n + 1) * W], w, sd[:, n, :], ALU.mult, ALU.mult).then_inc(dst_ready, 1)


class Steps:

    def __init__(self, eng, sem):
        self.eng, self.sem, self.n = eng, sem, 0

    def __call__(self, ins):
        self.n += 1
        ins.then_inc(self.sem, 1)
        self.eng.wait_ge(self.sem, self.n)


def top_two(dve, step, values, best, where, wheref, iota, one_hot):
    rows, tiles = values.shape[0], values.shape[1]
    for t in range(tiles):
        step(dve.max(best[:, t, :], values[:, t, :]))
        step(dve.max_index(where[:, t, :], best[:, t, :], values[:, t, :]))
    step(dve.tensor_copy(wheref, where))
    io = iota.unsqueeze(1).to_broadcast([rows, tiles, E])
    for k in range(2):
        step(dve.tensor_tensor(one_hot[:, k, :, :], io, wheref[:, :, k:k + 1].to_broadcast([rows, tiles, E]), ALU.is_equal))


def moe_phase(nc, res, w, ph):
    HN, UPD = res["HN"], res["UPD"]
    tokens = res["tokens"]
    NT = tokens // ROWS
    W, N = chunks_of(tokens)
    G = E // 2 + 1
    units = [(n, q) for n in range(N) for q in range(G)]
    with ExitStack() as ctx:
        sem = phase_semaphores(nc, ctx, ph)
        sb = lambda n, s, d=F32: ctx.enter_context(nc.sbuf_tensor(ph + n, s, d))
        pb = lambda n, s: ctx.enter_context(nc.psum_tensor(ph + n, s, F32))
        wg = sb("wg", [C, G, C])
        wu = sb("wu", [C, G, C])
        wd = sb("wd", [C, G, C])
        wgate = sb("wgate", [C, E])
        ebias = sb("ebias", [ROWS, E])
        iota = sb("iota", [ROWS, E])
        probs = sb("probs", [ROWS, NT, E])
        stat = sb("stat", [ROWS, NT])
        best = sb("best", [ROWS, NT, 8])
        where = sb("where", [ROWS, NT, 8], U32)
        wheref = sb("wheref", [ROWS, NT, 8])
        one_hot = sb("one_hot", [ROWS, 2, NT, E])
        comb = sb("comb", [ROWS, NT, E + 1])
        comb_wide = sb("comb_wide", [ROWS, NT, (E + 1) * I0])
        sg = sb("sg", [C, 2, W])
        hid = sb("hid", [C, 2, W])
        g_ps = pb("g_ps", [C, 2, 512])
        u_ps = pb("u_ps", [C, 2, 512])
        c_ps = pb("c_ps", [C, 2, 512])
        y_ps = pb("y_ps", [C, 512])
        r_ps = pb("r_ps", [C, 512])
        w_dma = sem("w_dma")
        logits_done = sem("logits_done")
        max_off = sem("max_off")
        exp_ready = sem("exp_ready")
        route = sem("route")
        comb_ready = sem("comb_ready")
        wide_ready = sem("wide_ready")
        g_done = sem("g_done")
        sg_ready = sem("sg_ready")
        c_done = sem("c_done")
        hu_ready = sem("hu_ready")
        hid_ready = sem("hid_ready")
        y_done = sem("y_done")
        y_taken = sem("y_taken")
        block = ctx.enter_context(nc.Block())
        weights = [(wgate, w["wgate"]), (ebias, w["ebias"]), (iota, w["iota"]), (wg, w["wg"]), (wu, w["wu"]), (wd, w["wd"])]
        NW = 16 * len(weights)

        def width(q):
            return C if q < G - 1 else I0

        @block.sync
        def _(sp):
            for dst, src in weights:
                sp.dma_start(dst[tuple(slice(None) for _ in dst.shape)], src).then_inc(w_dma, 16)

        @block.tensor
        def _(pe):
            pe.wait_ge(w_dma, NW)
            for t in range(NT):
                mm = pe.matmul(r_ps[0:ROWS, t * E:(t + 1) * E], HN[:, t * ROWS:(t + 1) * ROWS], wgate[:, :], start=True, stop=True)
            mm.then_inc(logits_done, 1)

            def down(k):
                n, q = units[k]
                m = width(q)
                pe.wait_ge(hid_ready, k + 1)
                if q == 0 and n:
                    pe.wait_ge(y_taken, n)
                pe.matmul(y_ps[:, 0:W], wd[0:m, q, :], hid[0:m, k % 2, :], start=(q == 0), stop=(q == G - 1)).then_inc(y_done, 1)

            for k, (n, q) in enumerate(units):
                m = width(q)
                x = HN[:, n * W:(n + 1) * W]
                if k >= 2:
                    pe.wait_ge(hu_ready, k - 1)
                pe.matmul(g_ps[0:m, k % 2, 0:W], wg[:, q, 0:m], x, start=True, stop=True)
                pe.matmul(u_ps[0:m, k % 2, 0:W], wu[:, q, 0:m], x, start=True, stop=True).then_inc(g_done, 1)
                if k >= 2:
                    pe.wait_ge(hid_ready, k - 1)
                for tt in range(W // ROWS):
                    tile = n * (W // ROWS) + tt
                    if q == 0:
                        pe.wait_ge(wide_ready, tile + 1)
                    wide = comb_wide[:, tile, q * C:q * C + m]
                    mm = pe.transpose(c_ps[0:m, k % 2, tt * ROWS:(tt + 1) * ROWS], wide, res["ident"][0:ROWS, 0:ROWS])
                mm.then_inc(c_done, 1)
                if k:
                    down(k - 1)
            down(len(units) - 1)

        @block.gpsimd
        def _(pool):
            pool.wait_ge(comb_ready, 1)
            for t in range(NT):
                pool.tensor_copy(comb_wide[:, t, :].rearrange("r (e i) -> r e i", i=I0), comb[:, t, :].unsqueeze(2).to_broadcast([ROWS, E + 1, I0])).then_inc(wide_ready, 1)

        @block.scalar
        def _(act):
            act.wait_ge(max_off, 1)
            act.activation(probs[:, :, :], probs[:, :, :], ACT.Exp).then_inc(exp_ready, 1)
            for k, (n, q) in enumerate(units):
                m = width(q)
                act.wait_ge(g_done, k + 1)
                if k >= 2:
                    act.wait_ge(hu_ready, k - 1)
                act.activation(sg[0:m, k % 2, :], g_ps[0:m, k % 2, 0:W], ACT.Silu).then_inc(sg_ready, 1)

        @block.vector
        def _(dve):
            step = Steps(dve, route)
            each = lambda v: v.unsqueeze(2).to_broadcast([ROWS, NT, E])
            dve.wait_ge(w_dma, NW)
            dve.wait_ge(logits_done, 1)
            step(dve.tensor_tensor(probs[:, :, :], r_ps[0:ROWS, 0:NT * E].rearrange("r (t e) -> r t e", e=E), ebias[:, :].unsqueeze(1).to_broadcast([ROWS, NT, E]), ALU.add))
            step(dve.tensor_reduce(stat[:, :], probs[:, :, :], AX.X, ALU.max))
            dve.tensor_tensor(probs[:, :, :], probs[:, :, :], each(stat[:, :]), ALU.subtract).then_inc(max_off, 1)
            dve.wait_ge(exp_ready, 1)
            step(dve.tensor_reduce(stat[:, :], probs[:, :, :], AX.X, ALU.add))
            step(dve.reciprocal(stat[:, :], stat[:, :]))
            step(dve.tensor_tensor(probs[:, :, :], probs[:, :, :], each(stat[:, :]), ALU.mult))
            top_two(dve, step, probs[:, :, :], best[:, :, :], where[:, :, :], wheref[:, :, :], iota[:, :], one_hot[:, :, :, :])
            step(dve.tensor_tensor(stat[:, :], best[:, :, 0], best[:, :, 1], ALU.add))
            step(dve.reciprocal(stat[:, :], stat[:, :]))
            step(dve.tensor_tensor(one_hot[:, 0, :, :], one_hot[:, 0, :, :], one_hot[:, 1, :, :], ALU.add))
            step(dve.tensor_tensor(probs[:, :, :], probs[:, :, :], one_hot[:, 0, :, :], ALU.mult))
            step(dve.memset(comb[:, :, E:E + 1], 1.0))
            dve.tensor_tensor(comb[:, :, 0:E], probs[:, :, :], each(stat[:, :]), ALU.mult).then_inc(comb_ready, 1)

            def take(n):
                dve.wait_ge(y_done, (n + 1) * G)
                cols = slice(n * W, (n + 1) * W)
                dve.tensor_tensor(UPD[:, cols], UPD[:, cols], y_ps[:, 0:W], ALU.add).then_inc(y_taken, 1)

            for k, (n, q) in enumerate(units):
                m = width(q)
                dve.wait_ge(sg_ready, k + 1)
                if k >= 2:
                    dve.wait_ge(y_done, k - 1)
                dve.tensor_tensor(hid[0:m, k % 2, :], sg[0:m, k % 2, :], u_ps[0:m, k % 2, 0:W], ALU.mult).then_inc(hu_ready, 1)
                dve.wait_ge(hu_ready, k + 1)
                dve.wait_ge(c_done, k + 1)
                dve.tensor_tensor(hid[0:m, k % 2, :], hid[0:m, k % 2, :], c_ps[0:m, k % 2, 0:W], ALU.mult).then_inc(hid_ready, 1)
                if q == 0 and n:
                    take(n - 1)
            take(N - 1)


def expert_ffn_phase(nc, res, w, ph):
    XN, UPD = res["XN"], res["UPD"]
    tokens, B = res["tokens"], res["B"]
    W, N = chunks_of(tokens)
    BW = W // T
    with ExitStack() as ctx:
        sem = phase_semaphores(nc, ctx, ph)
        sb = lambda n, s, d=F32: ctx.enter_context(nc.sbuf_tensor(ph + n, s, d))
        pb = lambda n, s: ctx.enter_context(nc.psum_tensor(ph + n, s, F32))
        w1 = sb("w1", [C, E, F1])
        w2 = sb("w2", [C, E, FB, C])
        b1 = sb("b1", [C, E, FB])
        b2 = sb("b2", [C, E])
        wr = sb("wr", [C, E])
        iota = sb("iota", [C, E])
        ones = sb("ones", [B, C])
        pooled = sb("pooled", [C, B])
        lg = sb("lg", [B, 1, E])
        best = sb("best", [B, 1, 8])
        where = sb("where", [B, 1, 8], U32)
        wheref = sb("wheref", [B, 1, 8])
        one_hot = sb("one_hot", [B, 2, 1, E])
        wt = sb("wt", [B, 4])
        comb = sb("comb", [B, E])
        diag = sb("diag", [B, E, B])
        cw = sb("cw", [C, E, B])
        hs = sb("hs", [C, 2, FB, W])
        part = sb("part", [C, 2, W])
        h_ps = pb("h_ps", [C, FB, 512])
        y_ps = pb("y_ps", [C, 2, 512])
        r_ps = pb("r_ps", [C, 512])
        w_dma = sem("w_dma")
        route = sem("route")
        pooled_ready = sem("pooled_ready")
        logits_done = sem("logits_done")
        diff_ready = sem("diff_ready")
        exp_ready = sem("exp_ready")
        diag_ready = sem("diag_ready")
        spread = sem("spread")
        cw_ready = sem("cw_ready")
        h_done = sem("h_done")
        hs_ready = sem("hs_ready")
        y_done = sem("y_done")
        y_taken = sem("y_taken")
        added = sem("added")
        block = ctx.enter_context(nc.Block())
        small = [(wr, w["wr"]), (iota, w["iota1"]), (b1, w["b1"]), (b2, w["b2"])]
        NW = 16 * (len(small) + 2)

        @block.sync
        def _(sp):
            for dst, src in small + [(w1, w["w1"]), (w2, w["w2"])]:
                sp.dma_start(dst[tuple(slice(None) for _ in dst.shape)], src).then_inc(w_dma, 16)

        def over_chunks(eng, chunk):
            chunk(0, True)
            if N > 1:
                with eng.Fori(1, N) as n:
                    chunk(n, False)

        @block.tensor
        def _(pe):
            pe.wait_ge(w_dma, NW)
            pe.wait_ge(pooled_ready, 1)
            pe.matmul(r_ps[0:B, 0:E], pooled[:, :], wr[:, :], start=True, stop=True).then_inc(logits_done, 1)
            pe.wait_ge(diag_ready, 1)
            pe.matmul(r_ps[:, 0:E * B], ones[:, :], diag[:, :, :].rearrange("b e c -> b (e c)"), start=True, stop=True).then_inc(spread, 1)

            def up(n, e, first):
                x = XN[:, bass.ds(n * W, W)]
                for f in range(FB):
                    if not (first and e == 0):
                        pe.wait_ge(hs_ready, FB * (E * n + e - 1) + f + 1)
                    pe.matmul(h_ps[:, f, 0:W], w1[:, e, f * C:(f + 1) * C], x, start=True, stop=True).then_inc(h_done, 1)

            def down(n, e, first):
                pe.wait_ge(hs_ready, FB * (E * n + e) + FB)
                if not (first and e < 2):
                    pe.wait_ge(y_taken, E * n + e - 1)
                for f in range(FB):
                    mm = pe.matmul(y_ps[:, e % 2, 0:W], w2[:, e, f, :], hs[:, e % 2, f, :], start=(f == 0), stop=(f == FB - 1))
                mm.then_inc(y_done, 1)

            def chunk(n, first):
                for e in range(E):
                    up(n, e, first)
                    if e:
                        down(n, e - 1, first)
                    elif not first:
                        down(n - 1, E - 1, False)

            over_chunks(pe, chunk)
            down(N - 1, E - 1, False)

        @block.scalar
        def _(act):
            act.wait_ge(diff_ready, 1)
            act.activation(wt[:, 0:1], wt[:, 0:1], ACT.Exp).then_inc(exp_ready, 1)
            act.wait_ge(w_dma, NW)

            def chunk(n, first):
                for e in range(E):
                    for f in range(FB):
                        act.wait_ge(h_done, FB * (E * n + e) + f + 1)
                        if f == 0 and not (first and e < 2):
                            act.wait_ge(y_done, E * n + e - 1)
                        act.activation(hs[:, e % 2, f, :], h_ps[:, f, 0:W], ACT.Gelu, bias=b1[:, e, f:f + 1]).then_inc(hs_ready, 1)

            over_chunks(act, chunk)

        @block.vector
        def _(dve):
            step = Steps(dve, route)
            step(dve.memset(ones[:, :], 1.0))
            step(dve.memset(wt[:, :], 0.0))
            step(dve.tensor_reduce(pooled[:, :], XN[:, :].rearrange("c (b t) -> c b t", t=T), AX.X, ALU.add))
            dve.tensor_scalar(pooled[:, :], pooled[:, :], 1.0 / T, None, ALU.mult).then_inc(pooled_ready, 1)
            dve.wait_ge(w_dma, NW)
            dve.wait_ge(logits_done, 1)
            step(dve.tensor_copy(lg[:, 0, :], r_ps[0:B, 0:E]))
            top_two(dve, step, lg[:, :, :], best[:, :, :], where[:, :, :], wheref[:, :, :], iota[0:B, :], one_hot[:, :, :, :])
            dve.tensor_tensor(wt[:, 0:1], best[:, 0, 1:2], best[:, 0, 0:1], ALU.subtract).then_inc(diff_ready, 1)
            dve.wait_ge(exp_ready, 1)
            step(dve.tensor_scalar(wt[:, 1:2], wt[:, 0:1], 1.0, None, ALU.add))
            step(dve.reciprocal(wt[:, 2:3], wt[:, 1:2]))
            step(dve.tensor_tensor(wt[:, 3:4], wt[:, 0:1], wt[:, 2:3], ALU.mult))
            step(dve.tensor_scalar(comb[:, :], one_hot[:, 0, 0, :], wt[:, 2:3], None, ALU.mult))
            step(dve.scalar_tensor_tensor(comb[:, :], one_hot[:, 1, 0, :], wt[:, 3:4], comb[:, :], ALU.mult, ALU.add))
            dve.tensor_tensor(diag[:, :, :], comb[:, :].unsqueeze(2).to_broadcast([B, E, B]), res["ident"][0:B, 0:B].unsqueeze(1).to_broadcast([B, E, B]), ALU.mult).then_inc(diag_ready, 1)
            dve.wait_ge(spread, 1)
            dve.tensor_copy(cw[:, :, :], r_ps[:, 0:E * B].rearrange("c (e b) -> c e b", b=B)).then_inc(cw_ready, 1)
            dve.wait_ge(cw_ready, 1)

            def chunk(n, first):
                cols = bass.ds(n * W, W)
                for e in range(E):
                    k = E * n + e
                    dve.wait_ge(y_done, k + 1)
                    weight = cw[:, e, bass.ds(n * BW, BW)].unsqueeze(2).to_broadcast([C, BW, T])
                    y3 = y_ps[:, e % 2, 0:W].rearrange("c (b t) -> c b t", t=T)
                    dst = UPD[:, cols] if e == 0 else part[:, e % 2, :]
                    if e >= 2:
                        dve.wait_ge(added, (E - 1) * n + e - 2)
                    dve.scalar_tensor_tensor(dst.rearrange("c (b t) -> c b t", t=T), y3, b2[:, e:e + 1], weight, ALU.add, ALU.mult).then_inc(y_taken, 1)
                    dve.wait_ge(y_taken, k + 1)
                    if e:
                        if e >= 2:
                            dve.wait_ge(added, (E - 1) * n + e - 1)
                        dve.tensor_tensor(UPD[:, cols], UPD[:, cols], part[:, e % 2, :], ALU.add).then_inc(added, 1)

            over_chunks(dve, chunk)


def store_phase(nc, res, gate, out, ph):
    XT, UPD = res["XT"], res["UPD"]
    W, N = chunks_of(res["tokens"])
    with ExitStack() as ctx:
        sem = phase_semaphores(nc, ctx, ph)
        x_ready = sem("x_ready")
        stored = sem("stored")
        block = ctx.enter_context(nc.Block())

        @block.vector
        def _(dve):
            for n in range(N):
                cols = slice(n * W, (n + 1) * W)
                dve.scalar_tensor_tensor(XT[:, cols], UPD[:, cols], gate, XT[:, cols], ALU.mult, ALU.add).then_inc(x_ready, 1)

        @block.sync
        def _(sp):
            for n in range(N):
                sp.wait_ge(x_ready, n + 1)
                sp.dma_start(out[:, n * W:(n + 1) * W], XT[:, n * W:(n + 1) * W]).then_inc(stored, 16)
            sp.wait_ge(stored, 16 * N)


def self_attention_phase(nc, res, w, ph):
    XN, HN, UPD = res["XN"], res["HN"], res["UPD"]
    NT = res["B"] // 2
    Q = 2 * NOPE + 2 * ROPE
    with ExitStack() as ctx:
        sem = phase_semaphores(nc, ctx, ph)
        sb = lambda n, s, d=F32: ctx.enter_context(nc.sbuf_tensor(ph + n, s, d))
        pb = lambda n, s: ctx.enter_context(nc.psum_tensor(ph + n, s, F32))
        wcos = sb("wcos", [C, PAIRS + 1, C])
        wsin = sb("wsin", [C, PAIRS + 1, C])
        wqn = sb("wqn", [2 * NOPE, PAIRS, C])
        wkvb = sb("wkvb", [2 * NOPE, PAIRS, 2 * RANK])
        wo = sb("wo", [2 * NOPE, PAIRS, C])
        wlat = sb("wlat", [C, 2 * RANK])
        tabs = sb("tabs", [C, 2, T])
        causal = sb("causal", [C, T])
        latsel = sb("latsel", [ROWS, 2 * RANK])
        wout = sb("wout", [C, 2, C])
        hs2 = sb("hs2", [C, 2, 2, 2, T])
        tc_ = sb("tc", [C, 2, 4, ROWS])
        ts_ = sb("ts", [C, 2, 4, ROWS])
        tck = sb("tck", [C, ROWS])
        tsk = sb("tsk", [C, ROWS])
        qp = sb("qp", [C, 2, PAIRS, ROWS + 8])
        kblk = sb("kblk", [C, 2, 2, ROWS])
        latb = sb("latb", [ROWS, 3, 2, 2 * RANK])
        s_sb = sb("s_sb", [C, 2, HF * T])
        mx = sb("mx", [C, 2, HF])
        rs = sb("rs", [C, 2, HF])
        pT = sb("pT", [ROWS, 2, PAIRS * C])
        uT = sb("uT", [C, 2, 2 * ROWS])
        proj_ps = pb("proj_ps", [C, 4, 512])
        key_ps = pb("key_ps", [C, 512])
        s_ps = pb("s_ps", [C, 2, 512])
        u_ps = pb("u_ps", [C, 512])

        w_dma = sem("w_dma")
        zeroed = sem("zeroed")
        fold_done = sem("fold_done")
        folded = sem("folded")
        hs_ready = sem("hs_ready")
        proj_done = sem("proj_done")
        key_done = sem("key_done")
        rot_a = sem("rot_a")
        rot_b = sem("rot_b")
        q_ready = sem("q_ready")
        rot_k = sem("rot_k")
        lat_ready = sem("lat_ready")
        k_ready = sem("k_ready")
        s_done = sem("s_done")
        s_taken = sem("s_taken")
        mx_ready = sem("mx_ready")
        sub_ready = sem("sub_ready")
        e_ready = sem("e_ready")
        sum_ready = sem("sum_ready")
        rec_ready = sem("rec_ready")
        p_ready = sem("p_ready")
        pT_done = sem("pT_done")
        pT_ready = sem("pT_ready")
        u_done = sem("u_done")
        u_ready = sem("u_ready")
        out_done = sem("out_done")
        out_taken = sem("out_taken")
        block = ctx.enter_context(nc.Block())
        weights = [(wcos, w["wcos"]), (wsin, w["wsin"]), (wqn, w["wqn"]), (wkvb, w["wkvb"]), (wo, w["wo0"]),
                   (wlat, w["wlat"]), (tabs, w["tabs"]), (causal, w["causal"]), (latsel, w["latsel"])]
        NW = 16 * len(weights)

        def over_tiles(eng, tile):
            for i in range(min(2, NT // 2)):
                tile(i, 0)
                tile(i, 1)
            if NT > 4:
                with eng.Fori(2, NT // 2) as i:
                    tile(i, 0)
                    tile(i, 1)

        def first(i):
            return isinstance(i, int) and i == 0

        @block.sync
        def _(sp):
            for dst, src in weights:
                sp.dma_start(dst[tuple(slice(None) for _ in dst.shape)], src).then_inc(w_dma, 16)

        @block.gpsimd
        def _(pool):
            pool.memset(qp[:, :, :, :], 0.0).then_inc(zeroed, 1)
            pool.memset(kblk[:, :, :, :], 0.0).then_inc(zeroed, 1)
            pool.wait_ge(zeroed, 2)

            def tile(i, s):
                n = 2 * i + s
                if not first(i):
                    pool.wait_ge(key_done, n - 1)
                src = HN[:, bass.ds(n * ROWS, ROWS)].rearrange("c (b t) -> c b t", t=T)
                for twice in range(2):
                    ins = pool.tensor_copy(hs2[:, s, :, twice, :], src)
                ins.then_inc(hs_ready, 1)
                pool.wait_ge(rot_k, 2 * n + 2)
                if not first(i):
                    pool.wait_ge(s_done, n - 1)
                for b in range(2):
                    for hh in range(2):
                        half = slice(64 * hh, 64 * hh + 64)
                        pool.tensor_tensor(kblk[half, s, b, hh * T:hh * T + T], tck[half, b * T:b * T + T], tsk[half, b * T:b * T + T], ALU.add).then_inc(k_ready, 1)
                pool.wait_ge(k_ready, 4 * n + 4)
                for half in range(2):
                    pool.wait_ge(rot_b, 2 * n + half + 1)
                    g = 4 * (1 - half)
                    pool.tensor_tensor(qp[:, s, g:g + 4, 0:ROWS], tc_[:, half, :, :], ts_[:, half, :, :], ALU.add).then_inc(q_ready, 1)

            over_tiles(pool, tile)

        @block.tensor
        def _(pe):
            pe.wait_ge(w_dma, NW)
            for p in range(PAIRS):
                pe.matmul(key_ps[:, p * 2 * RANK:(p + 1) * 2 * RANK], wqn[:, p, :], wkvb[:, p, :], start=True, stop=True)
            for p in range(PAIRS):
                g = 32 * (p % 4)
                mm = pe.matmul(u_ps[g:g + 32, (p // 4) * C:(p // 4 + 1) * C], wkvb[:, p, :], wo[:, p, :], start=True, stop=True)
            mm.then_inc(fold_done, 1)
            pe.wait_ge(folded, 2)

            def turn(i, s):
                n = 2 * i + s
                pe.wait_ge(p_ready, n + 1)
                for p in range(PAIRS):
                    mm = pe.transpose(proj_ps[0:ROWS, p // 4, (p % 4) * C:(p % 4 + 1) * C], s_sb[:, s, p * ROWS:(p + 1) * ROWS], res["ident"][:, :])
                mm.then_inc(pT_done, 1)

            def project(i, s, turned):
                n = 2 * i + s
                tokens = HN[:, bass.ds(n * ROWS, ROWS)]
                for half in range(2):
                    if not (first(i) and s == 0):
                        pe.wait_ge(rot_b, 2 * n - 1 + half)
                    if half == 1 and turned is not None:
                        pe.wait_ge(pT_ready, turned + 1)
                    bank = 2 * (1 - half)
                    for k, wt in enumerate((wcos, wsin)):
                        for pp in range(4):
                            mm = pe.matmul(proj_ps[:, bank + k, pp * ROWS:(pp + 1) * ROWS], wt[:, 4 * (1 - half) + pp, :], tokens, start=True, stop=True)
                    mm.then_inc(proj_done, 1)
                    if half == 0:
                        pe.wait_ge(hs_ready, n + 1)
                        if not (first(i) and s == 0):
                            pe.wait_ge(lat_ready, 2 * n)
                        for k, wt in enumerate((wcos, wsin)):
                            pe.matmul(key_ps[:, k * ROWS:(k + 1) * ROWS], wt[:, PAIRS, :], tokens, start=True, stop=True)
                        for b in range(2):
                            mm = pe.matmul(key_ps[0:ROWS, 256 + b * 2 * RANK:256 + (b + 1) * 2 * RANK], hs2[:, s, b, :, :].rearrange("c a t -> c (a t)"), wlat[:, :], start=True, stop=True)
                        mm.then_inc(key_done, 1)

            def scores(i, s):
                n = 2 * i + s
                pe.wait_ge(q_ready, 2 * n + 2)
                pe.wait_ge(k_ready, 4 * n + 4)
                if not (first(i) and s == 0):
                    pe.wait_ge(s_taken, n)
                for p in range(PAIRS):
                    for b in range(2):
                        mm = pe.matmul(s_ps[64 * b:64 * b + 64, p // 4, (p % 4) * ROWS:(p % 4 + 1) * ROWS], qp[:, s, p, b * T:b * T + 64], kblk[:, s, b, :], start=True, stop=True)
                mm.then_inc(s_done, 1)

            def finish(i, s, lat):
                n = 2 * i + s
                pe.wait_ge(pT_ready, n + 1)
                if not (first(i) and s == 0):
                    pe.wait_ge(out_taken, n)
                for pg in range(2):
                    for b in range(2):
                        for g in range(4):
                            p = 4 * pg + g
                            mm = pe.matmul(u_ps[32 * g:32 * g + 32, pg * ROWS + b * T:pg * ROWS + b * T + T], latb[:, s, b, :], pT[:, s, p * C + 64 * b:p * C + 64 * b + T], start=True, stop=True)
                mm.then_inc(u_done, 1)
                pe.wait_ge(u_ready, n + 1)
                for pg in range(2):
                    mm = pe.matmul(u_ps[:, 256:256 + ROWS], wout[:, pg, :], uT[:, s, pg * ROWS:(pg + 1) * ROWS], start=(pg == 0), stop=(pg == 1))
                mm.then_inc(out_done, 1)

            def tile(i, s):
                if not first(i):
                    turn(i - 1, s)
                project(i, s, None if first(i) else 2 * (i - 1) + s)
                if s == 1:
                    scores(i, 0)
                elif not first(i):
                    scores(i - 1, 1)
                if not first(i):
                    finish(i - 1, s, None)

            over_tiles(pe, tile)
            i = NT // 2 - 1
            turn(i, 0)
            scores(i, 1)
            finish(i, 0, None)
            turn(i, 1)
            finish(i, 1, None)

        @block.scalar
        def _(act):
            def exps(i, s):
                n = 2 * i + s
                act.wait_ge(sub_ready, n + 1)
                act.activation(s_sb[:, s, :], s_sb[:, s, :], ACT.Exp, scale=float(NOPE + ROPE) ** -0.5).then_inc(e_ready, 1)

            def take_turned(i, s):
                n = 2 * i + s
                act.wait_ge(pT_done, n + 1)
                if not first(i):
                    act.wait_ge(u_done, n - 1)
                act.activation(pT[:, s, :].rearrange("r (k w) -> r k w", k=2), proj_ps[0:ROWS, 0:2, :], ACT.Copy).then_inc(pT_ready, 1)

            def take_u(i, s):
                n = 2 * i + s
                act.wait_ge(u_done, n + 1)
                if not first(i):
                    act.wait_ge(out_done, n - 1)
                act.activation(uT[:, s, :], u_ps[:, 0:2 * ROWS], ACT.Copy).then_inc(u_ready, 1)

            def tile(i, s):
                if not first(i):
                    take_turned(i - 1, s)
                if s == 1:
                    exps(i, 0)
                elif not first(i):
                    exps(i - 1, 1)
                if not first(i):
                    take_u(i - 1, s)

            over_tiles(act, tile)
            i = NT // 2 - 1
            take_turned(i, 0)
            exps(i, 1)
            take_u(i, 0)
            take_turned(i, 1)
            take_u(i, 1)

        @block.vector
        def _(dve):
            dve.wait_ge(w_dma, NW)
            dve.wait_ge(fold_done, 1)
            dve.tensor_copy(wcos[:, 0:PAIRS, :].rearrange("c p (h x) -> c p h x", h=2)[:, :, :, 0:RANK], key_ps[:, 0:PAIRS * 2 * RANK].rearrange("c (p h r) -> c p h r", h=2, r=RANK)).then_inc(folded, 1)
            dve.tensor_copy(wout[:, :, :], u_ps[:, 0:2 * C].rearrange("x (g c) -> x g c", c=C)).then_inc(folded, 1)

            def table(k, reps):
                return tabs[:, k, :].unsqueeze(1).to_broadcast([C, reps, T])

            def rotate(i, s, half):
                n = 2 * i + s
                dve.wait_ge(proj_done, 2 * n + half + 1)
                if not (first(i) and s == 0):
                    dve.wait_ge(q_ready, 2 * n - 1 + half)
                for k, (dst, done) in enumerate(((tc_, rot_a), (ts_, rot_b))):
                    src = proj_ps[:, 2 * (1 - half) + k, 0:4 * ROWS].rearrange("c (m t) -> c m t", t=T)
                    dve.tensor_tensor(dst[:, half, :, :].rearrange("c p (b t) -> c (p b) t", t=T), src, table(k, 8), ALU.mult).then_inc(done, 1)

            def keys(i, s):
                n = 2 * i + s
                dve.wait_ge(key_done, n + 1)
                if not (first(i) and s == 0):
                    dve.wait_ge(k_ready, 4 * n)
                for k, dst in enumerate((tck, tsk)):
                    src = key_ps[:, k * ROWS:(k + 1) * ROWS].rearrange("c (b t) -> c b t", t=T)
                    dve.tensor_tensor(dst[:, :].rearrange("c (b t) -> c b t", t=T), src, table(k, 2), ALU.mult).then_inc(rot_k, 1)
                if not first(i):
                    dve.wait_ge(u_done, n - 1)
                for b in range(2):
                    dve.tensor_tensor(latb[:, s, b, :], key_ps[0:ROWS, 256 + b * 2 * RANK:256 + (b + 1) * 2 * RANK], latsel[:, :], ALU.mult).then_inc(lat_ready, 1)

            def softmax_front(i, s):
                n = 2 * i + s
                s3 = s_sb[:, s, :].rearrange("q (h t) -> q h t", t=T)
                dve.wait_ge(s_done, n + 1)
                if not first(i):
                    dve.wait_ge(pT_done, n - 1)
                dve.tensor_tensor(s_sb[:, s, :].rearrange("q (k h t) -> q k h t", k=2, t=T), s_ps[:, :, 0:4 * ROWS].rearrange("q k (h t) -> q k h t", t=T),
                                  causal[:, :].unsqueeze(1).unsqueeze(1).to_broadcast([C, 2, 8, T]), ALU.add).then_inc(s_taken, 1)
                dve.wait_ge(s_taken, n + 1)
                dve.tensor_reduce(mx[:, s, :], s3, AX.X, ALU.max).then_inc(mx_ready, 1)
                dve.wait_ge(mx_ready, n + 1)
                dve.tensor_tensor(s3, s3, mx[:, s, :].unsqueeze(2).to_broadcast([C, HF, T]), ALU.subtract).then_inc(sub_ready, 1)

            def softmax_back(i, s):
                n = 2 * i + s
                s3 = s_sb[:, s, :].rearrange("q (h t) -> q h t", t=T)
                dve.wait_ge(e_ready, n + 1)
                dve.tensor_reduce(rs[:, s, :], s3, AX.X, ALU.add).then_inc(sum_ready, 1)
                dve.wait_ge(sum_ready, n + 1)
                dve.reciprocal(rs[:, s, :], rs[:, s, :]).then_inc(rec_ready, 1)
                dve.wait_ge(rec_ready, n + 1)
                dve.tensor_tensor(s3, s3, rs[:, s, :].unsqueeze(2).to_broadcast([C, HF, T]), ALU.mult).then_inc(p_ready, 1)

            def take_out(i, s):
                n = 2 * i + s
                dve.wait_ge(out_done, n + 1)
                cols = bass.ds(n * ROWS, ROWS)
                dve.tensor_tensor(UPD[:, cols], u_ps[:, 256:256 + ROWS], XN[:, cols], ALU.add).then_inc(out_taken, 1)

            def tile(i, s):
                rotate(i, s, 0)
                keys(i, s)
                rotate(i, s, 1)
                if s == 1:
                    softmax_front(i, 0)
                    softmax_back(i, 0)
                elif not first(i):
                    softmax_front(i - 1, 1)
                    softmax_back(i - 1, 1)
                if not first(i):
                    take_out(i - 1, s)

            over_tiles(dve, tile)
            i = NT // 2 - 1
            softmax_front(i, 1)
            softmax_back(i, 1)
            take_out(i, 0)
            take_out(i, 1)


def constants_self_attention():
    f32 = np.float32
    freqs = (f32(1.0) / f32(THETA) ** (np.arange(0, ROPE * 1, 2, dtype=f32) / f32(ROPE))).astype(f32)
    ang = np.outer(np.arange(T, dtype=f32), freqs).astype(f32)
    cos, sin = np.cos(ang).T, np.sin(ang).T
    tabs = np.zeros((C, 2, T), f32)
    for base in (0, 64):
        tabs[base:base + RANK, 0] = 1.0
        tabs[base + RANK:base + KD, 0] = np.repeat(cos, 2, axis=0)
        tabs[base + RANK:base + KD:2, 1] = -sin
        tabs[base + RANK + 1:base + KD:2, 1] = sin
    causal = np.zeros((C, T), f32)
    for base in (0, 64):
        causal[base:base + T] = np.where(np.tril(np.ones((T, T), bool)), 0.0, -1.0e30)
    r = np.arange(ROWS)
    latsel = (r[:, None] // T == np.arange(2 * RANK)[None, :] // RANK).astype(f32)
    return {"tabs": tabs, "causal": causal, "latsel": latsel}


def lay_out_self_attention(Wq, Wkva, Wkvb, Wo):
    D = NOPE + ROPE
    q = Wq.reshape(C, PAIRS, 2, D)
    swap = np.arange(ROPE) ^ 1
    z = lambda *s: np.zeros(s, np.float32)
    wcos, wsin = z(C, PAIRS + 1, 2, 64), z(C, PAIRS + 1, 2, 64)
    wcos[:, :PAIRS, :, RANK:KD] = q[..., NOPE:]
    wsin[:, :PAIRS, :, RANK:KD] = q[..., NOPE:][..., swap]
    wcos[:, PAIRS, :, 0:KD] = Wkva[:, None, :]
    wsin[:, PAIRS, :, RANK:KD] = Wkva[:, None, RANK:][..., swap]
    wqn = q[..., :NOPE].transpose(2, 3, 1, 0).reshape(2 * NOPE, PAIRS, C)
    kvb = Wkvb.reshape(RANK, PAIRS, 2, NOPE)
    wkvb = z(2, NOPE, PAIRS, 2, RANK)
    for h in range(2):
        wkvb[h, :, :, h, :] = kvb[:, :, h, :].transpose(2, 1, 0)
    wo = Wo.reshape(PAIRS, 2, D, C)[:, :, :NOPE].transpose(1, 2, 0, 3).reshape(2 * NOPE, PAIRS, C)
    lat = Wkva[:, :RANK]
    c = np.ascontiguousarray
    return {"wcos": c(wcos.reshape(C, PAIRS + 1, C)), "wsin": c(wsin.reshape(C, PAIRS + 1, C)), "wqn": c(wqn), "wkvb": c(wkvb.reshape(2 * NOPE, PAIRS, 2 * RANK)),
            "wo0": c(wo), "wlat": c(np.concatenate([lat, lat], 1))}


def constants_xattn():
    c = np.arange(C)
    d = np.arange(2 * DH)
    rowsel = ((c[:, None] // T == d[None, :] // DH) & (c[:, None] < ROWS)).astype(np.float32)
    groupsum = (c[:, None] % 32 == d[None, :]).astype(np.float32)
    x = np.arange(SLOTS * 2 * DH)
    part = np.array(Q_PART)[x // (2 * DH)]
    qsel = (part[None, None, None, :] == np.arange(3)[None, :, None, None]) & (
        c[:, None, None, None] == np.arange(PAIRS)[None, None, :, None] * 2 * DH + (x % (2 * DH))[None, None, None, :])
    slothead = (x[:, None] // DH % 2 == np.arange(2)[None, :]).astype(np.float32)
    return {"ident": np.eye(C, dtype=np.float32), "rowsel": rowsel, "groupsum": groupsum, "slothead": slothead, "qsel": qsel.astype(np.float32)}


def lay_out_experts0(Wg, Wu, Wd, sWg, sWu, sWd):
    z = np.zeros((C, I0), np.float32)
    pair = lambda a: a.reshape(E // 2, 2, C, I0).transpose(2, 0, 1, 3).reshape(C, E // 2, C)
    up = lambda a, s: np.ascontiguousarray(np.concatenate([pair(a), np.concatenate([s[0], z], 1)[:, None]], 1))
    down = np.concatenate([Wd.reshape(E // 2, C, C).transpose(1, 0, 2), np.concatenate([sWd[0], z.T], 0)[:, None]], 1)
    return {"wg": up(Wg, sWg), "wu": up(Wu, sWu), "wd": np.ascontiguousarray(down)}


def build_program(nc, aps, out, B):
    tokens = B * T
    with ExitStack() as ctx:
        sb = lambda n, s: ctx.enter_context(nc.sbuf_tensor(n, s, F32))
        res = {"B": B, "tokens": tokens}
        for name, shape in (("XT", [C, tokens]), ("XN", [C, tokens]), ("UPD", [C, tokens]), ("HN", [C, tokens]), ("gates", [C, 4]), ("avg", [C, C]), ("eps", [C, 1]),
                            ("ident", [C, C]), ("slothead", [SLOTS * 2 * DH, 2]), ("rowsel", [C, 2 * DH]), ("groupsum", [C, 2 * DH]), ("rmsw", [C, 2])):
            res[name] = sb(name, shape)
        res["qsel"] = ctx.enter_context(nc.sbuf_tensor("qsel", [C, 3, PAIRS, SLOTS * 2 * DH], BF16))
        gate = lambda k: res["gates"][:, k:k + 1]
        load_phase(nc, res, aps, "p0_")
        norm_phase(nc, res, None, None, "p1_")
        xattn_phase(nc, res, {k: aps[k + "_0"] for k in ("qwT", "kwT", "vwT", "owT", "bias", "vb")} | {"ctxT": aps["ctxT"]}, aps["mask"], "p2_")
        norm_phase(nc, res, gate(0), (res["rmsw"][:, 0:1], res["HN"]), "p3_")
        self_attention_phase(nc, res, aps, "p4_")
        rms_phase(nc, res, res["UPD"], res["HN"], res["rmsw"][:, 1:2], "p5_")
        moe_phase(nc, res, aps, "p6_")
        norm_phase(nc, res, gate(2), None, "p7_")
        xattn_phase(nc, res, {k: aps[k + "_1"] for k in ("qwT", "kwT", "vwT", "owT", "bias", "vb")} | {"ctxT": aps["ctxT"]}, None, "p8_")
        norm_phase(nc, res, gate(1), None, "p9_")
        expert_ffn_phase(nc, res, aps, "p10_")
        store_phase(nc, res, gate(3), out, "p11_")


def lay_out(a):
    c = np.ascontiguousarray
    a = {k: np.asarray(v) for k, v in a.items()}
    B = a["x"].shape[0]
    o = {"xT": c(a["x"].reshape(B * T, C).T), "ctxT": c(a["ctx_1024"].transpose(0, 2, 1)), "mask": a["mask_BxSxS2_if1"]}
    o["gates"] = c(np.broadcast_to(np.concatenate([a["g_xattn"], a["g_ffn"]])[None, :], (C, 4)))
    for layer, names in ((0, ("qw", "kw", "vw", "ow", "qb", "kb", "vb", "ob")), (1, ("Wq", "Wk", "Wv", "Wo", "bq", "bk", "bv", "bo"))):
        qw, kw, vw, ow, qb, kb, vb, ob = (a[f"L{layer}_xattn_{n}"] for n in names)
        kw, kb = kw[KEY_ORDER], kb[KEY_ORDER]
        for n, m in (("qwT", qw), ("kwT", kw), ("vwT", vw), ("owT", ow)):
            o[f"{n}_{layer}"] = c(m.T)
        o[f"bias_{layer}"] = c(np.stack([qb, kb, ob], 1))
        o[f"vb_{layer}"] = c(np.broadcast_to(vb, (C, C)))
    f = lambda n: a["L0_ffn_" + n]
    o["rmsw"] = c(np.stack([f("w_ln1"), f("w_ln2")], 1))
    o |= lay_out_self_attention(f("Wq"), f("Wkva"), f("Wkvb"), f("Wo"))
    o |= lay_out_experts0(f("Wg"), f("Wu"), f("Wd"), f("sWg"), f("sWu"), f("sWd"))
    o["wgate"] = f("Wgate")
    o["ebias"] = c(np.broadcast_to(f("expert_bias"), (ROWS, E)))
    o["iota"] = c(np.broadcast_to(np.arange(E, dtype=np.float32), (ROWS, E)))
    f = lambda n: a["L1_ffn_" + n]
    o["wr"] = f("Wr")
    o["iota1"] = c(np.broadcast_to(np.arange(E, dtype=np.float32), (C, E)))
    o["w1"] = c(f("W1").transpose(1, 0, 2))
    o["w2"] = c(f("W2").reshape(E, FB, C, C).transpose(2, 0, 1, 3))
    o["b1"] = c(f("b1").reshape(E, FB, C).transpose(2, 0, 1))
    o["b2"] = c(f("b2").T)
    return o | constants_xattn() | constants_self_attention()


def kernel(**inputs):
    import concourse.bacc as bacc
    from concourse.bass_utils import run_bass_kernel_spmd

    arrays = lay_out(inputs)
    B = arrays["ctxT"].shape[0]
    nc = bacc.Bacc("TRN2", target_bir_lowering=False, num_devices=1)
    aps = {k: nc.dram_tensor("in_" + k, v.shape, mybir.dt.from_np(v.dtype), kind="ExternalInput").ap() for k, v in arrays.items()}
    out = nc.dram_tensor("outT", (C, B * T), F32, kind="ExternalOutput").ap()
    build_program(nc, aps, out, B)
    got = run_bass_kernel_spmd(nc, [{"in_" + k: v for k, v in arrays.items()}], core_ids=[0]).results[0]["outT"]
    return np.ascontiguousarray(got.T).reshape(B, T, C)
```

```python
from contextlib import ExitStack

import numpy as np

import concourse.bass as bass
from concourse import mybir

F32 = mybir.dt.float32
I32 = mybir.dt.int32
U32 = mybir.dt.uint32
BF16 = mybir.dt.bfloat16
ALU = mybir.AluOpType
ACT = mybir.ActivationFunctionType
AX = mybir.AxisListType

C = 128
T = 56
KEYS = 1500
H = 16
DH = C // H
PAIRS = H // 2
ROWS = 2 * T
KC = 125
KCH = KEYS // KC
SB = 3
SW = KEYS // SB
TB = KCH // SB
VB = 3
VJ = KCH // VB
MASKED = -2.0 ** 30
Q_PART = (0, 0, 1, 1, 0, 2)
K_PART = (0, 1, 0, 1, 2, 0)
SLOTS = len(Q_PART)
KEY_ORDER = np.arange(C).reshape(2, PAIRS // 2, 2 * DH).transpose(0, 2, 1).reshape(C)
EPS = 1e-5

HF = 16
NOPE = 32
ROPE = 32
RANK = 16
KD = RANK + ROPE
THETA = 100000.0
E = 8
I0 = 64
F1 = 512
FB = F1 // C


def chunks_of(tokens):
    w = 8 * T if tokens % (8 * T) == 0 else 2 * T
    return w, tokens // w


def phase_semaphores(nc, ctx, ph):
    mine = []

    def sem(name):
        mine.append(nc.alloc_semaphore(ph + name))
        return mine[-1]

    def close():
        nc.clear_and_free_semaphores(mine)
        nc.all_engine_barrier()

    ctx.callback(close)
    return sem


def norm_phase(nc, res, src_gate, want_rms, ph):
    XT, XN, UPD = res["XT"], res["XN"], res["UPD"]
    tokens = res["tokens"]
    W, N = chunks_of(tokens)
    with ExitStack() as ctx:
        sem = phase_semaphores(nc, ctx, ph)
        sb = lambda n, s: ctx.enter_context(nc.sbuf_tensor(ph + n, s, F32))
        assert N <= 4
        dev = sb("dev", [C, N, W])
        sq = sb("sq", [C, N, W])
        sd = sb("sd", [C, N, W])
        mean_ps = ctx.enter_context(nc.psum_tensor(ph + "mean", [C, N, 512], F32))
        var_ps = ctx.enter_context(nc.psum_tensor(ph + "var", [C, N, 512], F32))
        x_ready = sem("x_ready")
        mean_done = sem("mean_done")
        dev_ready = sem("dev_ready")
        sq_ready = sem("sq_ready")
        var_done = sem("var_done")
        sd_ready = sem("sd_ready")
        rstd_ready = sem("rstd_ready")
        xn_ready = sem("xn_ready")
        sq2_ready = sem("sq2_ready")
        ms_done = sem("ms_done")
        sd2_ready = sem("sd2_ready")
        rrms_ready = sem("rrms_ready")
        h_ready = sem("h_ready")
        block = ctx.enter_context(nc.Block())

        def cols(n):
            return slice(n * W, n * W + W)


        @block.tensor
        def _(pe):
            for n in range(N):
                if src_gate is not None:
                    pe.wait_ge(x_ready, n + 1)
                pe.matmul(mean_ps[:, n, 0:W], res["avg"][:, :], XT[:, cols(n)], start=True, stop=True).then_inc(mean_done, 1)
            for n in range(N):
                pe.wait_ge(sq_ready, n + 1)
                pe.matmul(var_ps[:, n, 0:W], res["avg"][:, :], sq[:, n, :], start=True, stop=True).then_inc(var_done, 1)
            if want_rms is not None:
                for n in range(N):
                    pe.wait_ge(sq2_ready, n + 1)
                    pe.matmul(mean_ps[:, n, 0:W], res["avg"][:, :], sq[:, n, :], start=True, stop=True).then_inc(ms_done, 1)

        @block.scalar
        def _(act):
            for n in range(N):
                act.wait_ge(dev_ready, n + 1)
                act.activation(sq[:, n, :], dev[:, n, :], ACT.Square).then_inc(sq_ready, 1)
            for n in range(N):
                act.wait_ge(var_done, n + 1)
                act.activation(sd[:, n, :], var_ps[:, n, 0:W], ACT.Sqrt, bias=res["eps"][:, 0:1]).then_inc(sd_ready, 1)
            if want_rms is not None:
                for n in range(N):
                    act.wait_ge(xn_ready, n + 1)
                    act.activation(sq[:, n, :], XN[:, cols(n)], ACT.Square).then_inc(sq2_ready, 1)
                for n in range(N):
                    act.wait_ge(ms_done, n + 1)
                    act.activation(sd[:, n, :], mean_ps[:, n, 0:W], ACT.Sqrt, bias=res["eps"][:, 0:1]).then_inc(sd2_ready, 1)

        @block.vector
        def _(dve):
            if src_gate is not None:
                for n in range(N):
                    dve.scalar_tensor_tensor(XT[:, cols(n)], UPD[:, cols(n)], src_gate, XT[:, cols(n)], ALU.mult, ALU.add).then_inc(x_ready, 1)
            for n in range(N):
                if src_gate is not None:
                    dve.wait_ge(x_ready, n + 1)
                dve.wait_ge(mean_done, n + 1)
                dve.tensor_tensor(dev[:, n, :], XT[:, cols(n)], mean_ps[:, n, 0:W], ALU.subtract).then_inc(dev_ready, 1)
            for n in range(N):
                dve.wait_ge(sd_ready, n + 1)
                dve.reciprocal(sd[:, n, :], sd[:, n, :]).then_inc(rstd_ready, 1)
                if n:
                    dve.wait_ge(rstd_ready, n)
                    dve.tensor_tensor(XN[:, cols(n - 1)], dev[:, n - 1, :], sd[:, n - 1, :], ALU.mult).then_inc(xn_ready, 1)
            dve.wait_ge(rstd_ready, N)
            dve.tensor_tensor(XN[:, cols(N - 1)], dev[:, N - 1, :], sd[:, N - 1, :], ALU.mult).then_inc(xn_ready, 1)
            if want_rms is not None:
                w, out = want_rms
                for n in range(N):
                    dve.wait_ge(sd2_ready, n + 1)
                    dve.reciprocal(sd[:, n, :], sd[:, n, :]).then_inc(rrms_ready, 1)
                for n in range(N):
                    dve.wait_ge(rrms_ready, n + 1)
                    dve.scalar_tensor_tensor(out[:, cols(n)], XN[:, cols(n)], w, sd[:, n, :], ALU.mult, ALU.mult).then_inc(h_ready, 1)


def load_phase(nc, res, ins, ph):
    with ExitStack() as ctx:
        sem = phase_semaphores(nc, ctx, ph)
        loaded = sem("loaded")
        made = sem("made")
        qsel32 = ctx.enter_context(nc.sbuf_tensor(ph + "qsel32", res["qsel"].shape, F32))
        block = ctx.enter_context(nc.Block())
        todo = [(res["XT"], ins["xT"]), (res["gates"], ins["gates"]), (res["ident"], ins["ident"]),
                (res["slothead"], ins["slothead"]), (res["rowsel"], ins["rowsel"]), (res["groupsum"], ins["groupsum"]), (res["rmsw"], ins["rmsw"])]

        @block.sync
        def _(sp):
            for dst, src in todo:
                sp.dma_start(dst[:, :], src).then_inc(loaded, 16)
            sp.dma_start(qsel32[:, :, :, :], ins["qsel"]).then_inc(loaded, 16)
            sp.wait_ge(loaded, 16 * (len(todo) + 1))

        @block.vector
        def _(dve):
            dve.memset(res["avg"][:, :], 1.0 / C).then_inc(made, 1)
            dve.memset(res["eps"][:, :], EPS).then_inc(made, 1)
            dve.wait_ge(loaded, 16 * (len(todo) + 1))
            dve.tensor_copy(res["qsel"][:, :, :, :], qsel32[:, :, :, :]).then_inc(made, 1)
            dve.tensor_copy(res["identb"][:, :], res["ident"][:, :]).then_inc(made, 1)

        @block.scalar
        def _(act):
            act.wait_ge(loaded, 16 * (len(todo) + 1))
            act.activation(res["gates"][:, :], res["gates"][:, :], ACT.Tanh).then_inc(made, 1)


def xattn_phase(nc, res, w, mask, ph):
    XN, UPD, B = res["XN"], res["UPD"], res["B"]
    tokens = res["tokens"]
    masked = mask is not None
    W, N = chunks_of(tokens)
    PARTS = SLOTS * 2 * DH
    DEPTH = PARTS + 2
    HALF = PAIRS // 2
    VD = 2 * DH + 1
    with ExitStack() as ctx:
        sem = phase_semaphores(nc, ctx, ph)
        sb = lambda n, s, d=F32: ctx.enter_context(nc.sbuf_tensor(ph + n, s, d))
        pb = lambda n, s: ctx.enter_context(nc.psum_tensor(ph + n, s, F32))
        q32 = UPD
        qpart = sb("qpart", [C, 3, tokens], BF16)
        wq = sb("wq", [C, C])
        wk = sb("wk", [C, C])
        wv = sb("wv", [C, C])
        wo = sb("wo", [C, C])
        bias = sb("bias", [C, 4])
        ctxT = sb("ctxT", [C, 2, KEYS])
        kpart = sb("kpart", [C, 3, KEYS], BF16)
        krest = sb("krest", [C, 2, SW])
        kpack = sb("kpack", [DEPTH, 2, PAIRS, KEYS], BF16)
        qpack = sb("qpack", [DEPTH, 2, PAIRS, 2, T], BF16)
        vx = sb("vx", [KC, 2, KCH, PAIRS, 32])
        ones = sb("ones", [C, 3 * C], BF16)
        scratch = sb("scratch", [ROWS, KEYS])
        mx = sb("mx", [ROWS, PAIRS])
        mpart = sb("mpart", [ROWS, PAIRS, 2], BF16)
        pT = sb("pT", [KC, 2, KCH * ROWS])
        rrow = sb("rrow", [ROWS, PAIRS])
        pv_sb = sb("pv_sb", [C, 2, 4 * ROWS])
        o_sel = sb("o_sel", [ROWS, PAIRS, 2 * DH])
        o_nrm = sb("o_nrm", [ROWS, PAIRS, 2 * DH])
        oT = sb("oT", [C, ROWS])
        zero = sb("zero", [C, 1])
        if masked:
            maskb = sb("maskb", [ROWS, 2, KEYS], I32)
            maskT = sb("maskT", [KC, KCH, T], I32)
            pen0 = sb("pen0", [KC, KCH, T], BF16)
            pen = sb("pen", [KC, 2, KCH, T], BF16)
            live = sb("live", [C, T])
            qlive = sb("qlive", [C, 3, T], BF16)
            rowlive = sb("rowlive", [ROWS, HALF])
            nmax = sb("nmax", [ROWS, HALF])
            carrier = sb("carrier", [ROWS, 1])
            pool_carrier = sb("pool_carrier", [C, 2])
        score_ps = pb("score_ps", [C, SB, 512])
        sT_ps = pb("sT_ps", [C, SB, 512])
        pv_ps = pb("pv_ps", [C, 512])
        misc_ps = pb("misc_ps", [C, 512])

        w_dma = sem("w_dma")
        set_up = sem("set_up")
        ones_dma = sem("ones_dma")
        q_done = sem("q_done")
        q32_ready = sem("q32_ready")
        q0_ready = sem("q0_ready")
        qrest_ready = sem("qrest_ready")
        q1_ready = sem("q1_ready")
        q2_ready = sem("q2_ready")
        ctx_dma = [sem("ctx_dma0"), sem("ctx_dma1")]
        k_done = sem("k_done")
        k32_ready = sem("k32_ready")
        k0_ready = sem("k0_ready")
        krest_ready = sem("krest_ready")
        k1_ready = sem("k1_ready")
        k2_ready = sem("k2_ready")
        kpack_dma = [[sem(f"kpack_dma{s}{h}") for h in range(2)] for s in range(2)]
        v_done = sem("v_done")
        v_ready = sem("v_ready")
        qpack_done = sem("qpack_done")
        qpack_ready = sem("qpack_ready")
        s_done = sem("s_done")
        s_taken = sem("s_taken")
        nmax_step = sem("nmax_step")
        mpart_ready = sem("mpart_ready")
        mT_done = sem("mT_done")
        mT_ready = sem("mT_ready")
        t_done = sem("t_done")
        p_ready = sem("p_ready")
        pv_done = sem("pv_done")
        pv_taken = sem("pv_taken")
        sel_done = sem("sel_done")
        recip_ready = sem("recip_ready")
        osel_ready = sem("osel_ready")
        onrm_ready = sem("onrm_ready")
        turn_done = sem("turn_done")
        oT_ready = sem("oT_ready")
        out_done = sem("out_done")
        out_taken = sem("out_taken")
        if masked:
            mask_dma = [sem("mask_dma0"), sem("mask_dma1")]
            maskT_dma = sem("maskT_dma")
            mask_ready = sem("mask_ready")
            pen0_ready = sem("pen0_ready")
            live_done = sem("live_done")
            live_ready = sem("live_ready")
            qlive_ready = sem("qlive_ready")
            pen_ready = sem("pen_ready")
            rowlive_ready = sem("rowlive_ready")
            nmax_ready = sem("nmax_ready")
        block = ctx.enter_context(nc.Block())

        def over_batches(eng, batch):
            pairs = B // 2

            def pair(i, first, last):
                batch(i, 0, first, False)
                batch(i, 1, False, last)

            pair(0, True, pairs == 1)
            if pairs > 2:
                with eng.Fori(1, pairs - 1) as i:
                    pair(i, False, False)
            if pairs > 1:
                pair(pairs - 1, False, True)

        def early(i):
            return isinstance(i, int) and i == 0

        @block.sync
        def _(sp):
            for dst, src in ((wq, w["qwT"]), (wk, w["kwT"]), (wv, w["vwT"]), (wo, w["owT"]), (bias, w["bias"])):
                sp.dma_start(dst[:, :], src).then_inc(w_dma, 16)

            def load_context(b, s):
                sp.dma_start(ctxT[:, s, :], w["ctxT"][bass.ds(b, 1), :, :].rearrange("a c k -> (a c) k")).then_inc(ctx_dma[s], 16)

            def load_mask(b, s):
                for half in range(2):
                    sp.dma_start(maskb[half * T:half * T + T, s, :], mask[bass.ds(b, 1), :, :].rearrange("a q k -> (a q) k")).then_inc(mask_dma[s], 16)

            def load_maskT(b):
                sp.dma_start(maskT[:, :, :], w["maskT"][bass.ds(b, 1), :, :, :].rearrange("a k j q -> (a k) j q")).then_inc(maskT_dma, 16)

            def pack_keys(s, half):
                for slot, part in enumerate(K_PART):
                    sp.dma_start(kpack[slot * 2 * DH:(slot + 1) * 2 * DH, s, half * HALF:(half + 1) * HALF, :],
                                 kpart[half * C // 2:(half + 1) * C // 2, part, :]).then_inc(kpack_dma[s][half], 16)

            load_context(0, 0)
            if masked:
                load_maskT(0)
            load_context(1, 1)
            sp.wait_ge(set_up, 4)
            sp.dma_start(kpack[PARTS:DEPTH, :, :, :], ones[:, 0:2 * 2 * PAIRS * KEYS // C]).then_inc(ones_dma, 16)
            if masked:
                load_mask(0, 0)
                load_mask(1, 1)
                sp.wait_ge(pen0_ready, 1)
                load_maskT(1)
            sp.wait_ge(k2_ready, SB)
            pack_keys(0, 0)
            pack_keys(0, 1)

            def batch(i, s, first, last):
                b = 2 * i + s
                final_pair = isinstance(i, int) and i == B // 2 - 1
                if not final_pair:
                    sp.wait_ge(v_done, SB * (b + 1))
                    load_context(b + 2, s)
                    if masked:
                        sp.wait_ge(pen0_ready, b + 2)
                        load_maskT(b + 2)
                if not last:
                    sp.wait_ge(k2_ready, SB * (b + 2))
                    pack_keys(1 - s, 0)
                    if not first:
                        sp.wait_ge(t_done, PAIRS * b)
                    pack_keys(1 - s, 1)
                if masked and not final_pair:
                    sp.wait_ge(s_taken, PAIRS * (b + 1))
                    load_mask(b + 2, s)

            over_batches(sp, batch)

        @block.gpsimd
        def _(pool):
            pool.memset(ones[:, :], 1.0).then_inc(set_up, 1)
            pool.memset(zero[:, :], 0.0).then_inc(set_up, 1)
            pool.memset(vx[:, :, :, :, 2 * DH:32], 0.0).then_inc(set_up, 1)
            pool.wait_ge(set_up, 3)
            pool.memset(vx[:, :, :, :, 2 * DH:VD], 1.0).then_inc(set_up, 1)
            pool.wait_ge(set_up, 4)

            def split_keys(b):
                for u in range(SB):
                    cols = slice(u * SW, (u + 1) * SW)
                    pool.wait_ge(krest_ready, SB * b + u + 1)
                    pool.tensor_tensor(kpart[:, 1, cols], krest[:, u % 2, :], zero[:, 0:1].to_broadcast([C, SW]), ALU.add).then_inc(k1_ready, 1)
                    pool.wait_ge(k1_ready, SB * b + u + 1)
                    pool.tensor_tensor(kpart[:, 2, cols], krest[:, u % 2, :], kpart[:, 1, cols], ALU.subtract).then_inc(k2_ready, 1)

            def make_mask(i, s, early_one):
                if not early_one:
                    pool.wait_ge(mask_ready, 2 * i + s)
                pool.wait_ge(mask_dma[s], 32 * (i + 1))
                pool.tensor_tensor(pool_carrier[:, 0:1], zero[:, :], zero[:, :], ALU.add)
                pool.tensor_scalar(maskb[:, s, :].bitcast(F32), maskb[:, s, :], 0.0, MASKED, ALU.is_equal, ALU.mult).then_inc(mask_ready, 1)

            def make_pen0(b):
                if not (isinstance(b, int) and b == 0):
                    pool.wait_ge(pen_ready, b)
                pool.wait_ge(maskT_dma, 16 * (b + 1))
                pool.tensor_tensor(pool_carrier[:, 1:2], zero[:, :], zero[:, :], ALU.add)
                pool.tensor_scalar(pen0[:, :, :], maskT[:, :, :], 0.0, MASKED, ALU.is_equal, ALU.mult).then_inc(pen0_ready, 1)

            def make_pen(b, s, free):
                pool.wait_ge(live_ready, b + 1)
                if free is not None:
                    pool.wait_ge(t_done, free)
                pool.tensor_tensor(pen[:, s, :, :], pen0[:, :, :], live[0:KC, :].unsqueeze(1).to_broadcast([KC, KCH, T]), ALU.mult).then_inc(pen_ready, 1)

            def batch(i, s, first, last):
                b = 2 * i + s
                if not last:
                    if masked:
                        make_pen0(b + 1)
                    split_keys(b + 1)
                    if masked:
                        make_mask(i + s, 1 - s, False)
                        make_pen(b + 1, 1 - s, None if first else PAIRS * b)

            if masked:
                make_pen0(0)
            split_keys(0)
            if masked:
                make_mask(0, 0, True)
                make_pen(0, 0, None)
            over_batches(pool, batch)

        @block.tensor
        def _(pe):
            def keys(b, s, u):
                pe.matmul(misc_ps[:, 0:SW], wk[:, :], ctxT[:, s, u * SW:(u + 1) * SW], start=True, stop=True).then_inc(k_done, 1)

            def taken_keys(b, u):
                pe.wait_ge(k32_ready, SB * b + u + 1)

            def values(s, u):
                for jj in range(VJ):
                    j = u * VJ + jj
                    mm = pe.matmul(misc_ps[0:KC, jj * C:(jj + 1) * C], ctxT[:, s, j * KC:(j + 1) * KC], wv[:, :], start=True, stop=True)
                mm.then_inc(v_done, 1)

            def sum_penalties(b):
                pe.wait_ge(pen0_ready, b + 1)
                for j in range(KCH):
                    mm = pe.matmul(misc_ps[:, 0:T], ones[0:KC, 0:C], pen0[:, j, :], start=(j == 0), stop=(j == KCH - 1))
                mm.then_inc(live_done, 1)

            def place_queries(b):
                if masked:
                    pe.wait_ge(qlive_ready, b + 1)
                for p in range(PAIRS):
                    for part in range(3):
                        x = qlive[:, part, :] if masked else qpart[:, part, bass.ds(b * T, T)]
                        mm = pe.matmul(misc_ps[0:PARTS, p * T:(p + 1) * T], res["qsel"][:, part, p, :], x, start=(part == 0), stop=(part == 2))
                mm.then_inc(qpack_done, 1)

            def turn_maxima(b, g):
                pe.wait_ge(mpart_ready, 2 * b + g + 1)
                for tt in range(HALF):
                    mm = pe.matmul(misc_ps[PARTS:DEPTH, tt * ROWS:(tt + 1) * ROWS], mpart[:, g * HALF + tt, :], res["identb"][0:ROWS, 0:ROWS], start=True, stop=True)
                mm.then_inc(mT_done, 1)

            def row_scores(i, s, t, first):
                b = 2 * i + s
                if t == 0:
                    pe.wait_ge(qpack_ready, 2 * b + 2)
                if t % HALF == 0:
                    pe.wait_ge(kpack_dma[s][t // HALF], 16 * SLOTS * (i + 1))
                if not (first and t == 0):
                    pe.wait_ge(s_taken, PAIRS * b + t)
                for k in range(SB):
                    mm = pe.matmul(score_ps[0:ROWS, k, 0:SW], qpack[0:PARTS, s, t, :, :].rearrange("x h q -> x (h q)"), kpack[0:PARTS, s, t, k * SW:(k + 1) * SW], start=True, stop=True)
                mm.then_inc(s_done, 1)

            def key_scores(b, s, t, first):
                if t % HALF == 0:
                    pe.wait_ge(mT_ready, 2 * b + t // HALF + 1)
                    if masked and t == 0:
                        pe.wait_ge(pen_ready, b + 1)
                if not (first and t == 0):
                    pe.wait_ge(p_ready, PAIRS * b + t)
                for k in range(SB):
                    if masked:
                        pe.matmul(sT_ps[0:KC, k, 0:TB * ROWS].rearrange("x (j h q) -> x j h q", h=2, q=T), res["identb"][0:KC, 0:KC],
                                  pen[:, s, k * TB:(k + 1) * TB, :].unsqueeze(2).to_broadcast([KC, TB, 2, T]), start=True, stop=False)
                    for jj in range(TB):
                        j = k * TB + jj
                        mm = pe.matmul(sT_ps[0:KC, k, jj * ROWS:(jj + 1) * ROWS], kpack[:, s, t, j * KC:(j + 1) * KC], qpack[:, s, t, :, :].rearrange("x h q -> x (h q)"),
                                       start=not masked, stop=(not masked or jj == TB - 1))
                mm.then_inc(t_done, 1)

            def weigh(b, s, t, first):
                pe.wait_ge(p_ready, PAIRS * b + t + 1)
                if t == 0:
                    pe.wait_ge(v_ready, SB * (b + 1))
                    if not first:
                        pe.wait_ge(pv_taken, 2 * b)
                if t == HALF:
                    pe.wait_ge(pv_taken, 2 * b + 1)
                for j in range(KCH):
                    g = j % 4
                    mm = pe.matmul(pv_ps[32 * g:32 * g + 32, (t % HALF) * ROWS:(t % HALF + 1) * ROWS], vx[:, s, j, t, :], pT[:, t % 2, j * ROWS:(j + 1) * ROWS], start=(j < 4), stop=(j >= KCH - 4))
                mm.then_inc(pv_done, 1)

            def select(b):
                pe.wait_ge(pv_taken, 2 * b + 2)
                for t in range(PAIRS):
                    mm = pe.matmul(misc_ps[0:ROWS, t * VD:(t + 1) * VD], pv_sb[:, t // HALF, (t % HALF) * ROWS:(t % HALF + 1) * ROWS], res["groupsum"][:, :], start=True, stop=True)
                mm.then_inc(sel_done, 1)

            def turn(b):
                pe.wait_ge(onrm_ready, b + 1)
                pe.transpose(misc_ps[:, 0:ROWS], o_nrm[:, :, :].rearrange("r p d -> r (p d)"), res["ident"][0:ROWS, 0:ROWS]).then_inc(turn_done, 1)

            def project(b):
                pe.wait_ge(oT_ready, b + 1)
                pe.matmul(misc_ps[:, 0:T], wo[:, :], oT[:, 0:T], start=True, stop=False)
                pe.matmul(misc_ps[:, 0:T], wo[:, :], oT[:, T:ROWS], start=False, stop=True).then_inc(out_done, 1)

            def batch(i, s, first, last):
                b = 2 * i + s
                for t in range(PAIRS):
                    if t == 0 and not last:
                        pe.wait_ge(ctx_dma[1 - s], 16 * (i + 1 + s))
                        pe.wait_ge(qpack_ready, 2 * b + 2)
                        if not early(i):
                            pe.wait_ge(out_taken, b - 1)
                        keys(b + 1, 1 - s, 0)
                    if t == 1 and not last:
                        if first:
                            taken_keys(b + 1, 0)
                        else:
                            pe.wait_ge(mT_ready, 2 * b)
                        keys(b + 1, 1 - s, 1)
                    if t == 2 and not last:
                        pe.wait_ge(v_ready, SB * b + 1)
                        keys(b + 1, 1 - s, 2)
                    if t == 3:
                        if last:
                            pe.wait_ge(v_ready, SB * b + 1)
                        else:
                            taken_keys(b + 1, 2)
                        values(s, 1)
                    if t == 4:
                        if masked and not last:
                            pe.wait_ge(live_ready, b + 2)
                        else:
                            pe.wait_ge(v_ready, SB * b + 2)
                        values(s, 2)
                    if t == 5 and not last:
                        pe.wait_ge(mT_ready, 2 * b + 1)
                        place_queries(b + 1)
                    if t == 6 and not first:
                        if last:
                            pe.wait_ge(mT_ready, 2 * b + 1)
                        else:
                            pe.wait_ge(qpack_ready, 2 * b + 4)
                        select(b - 1)
                    if t == 7 and not first:
                        project(b - 1)
                    row_scores(i, s, t, first)
                    if t >= 6:
                        weigh(b, s, t - 6, first)
                    elif not first:
                        weigh(b - 1, 1 - s, t + PAIRS - 6, False)
                    if t == 0 and not first:
                        if not last:
                            taken_keys(b + 1, 0)
                        elif not early(i):
                            pe.wait_ge(out_taken, b - 1)
                        turn_maxima(b - 1, 1)
                    if t == 1:
                        if last:
                            pe.wait_ge(mT_ready, 2 * b)
                        else:
                            taken_keys(b + 1, 1)
                        values(s, 0)
                    if t == 3 and masked and not last:
                        pe.wait_ge(v_ready, SB * b + 2)
                        sum_penalties(b + 1)
                    if t == 4:
                        pe.wait_ge(v_ready, SB * b + 3)
                        turn_maxima(b, 0)
                    if t == 6 and not first:
                        turn(b - 1)
                    if t >= 5:
                        key_scores(b, s, t - 5, first)
                    elif not first:
                        key_scores(b - 1, 1 - s, t + PAIRS - 5, False)

            pe.wait_ge(w_dma, 16 * 5)
            for n in range(N):
                if n >= 1:
                    pe.wait_ge(q32_ready, n)
                pe.matmul(misc_ps[:, 0:W], wq[:, :], XN[:, n * W:(n + 1) * W], start=True, stop=True).then_inc(q_done, 1)
            pe.wait_ge(q32_ready, N)
            pe.wait_ge(ctx_dma[0], 16)
            for u in range(SB):
                if u:
                    taken_keys(0, u - 1)
                keys(0, 0, u)
            taken_keys(0, SB - 1)
            pe.wait_ge(q2_ready, N)
            if masked:
                sum_penalties(0)
                pe.wait_ge(live_ready, 1)
            place_queries(0)
            pe.wait_ge(set_up, 4)
            pe.wait_ge(ones_dma, 16)
            over_batches(pe, batch)
            b = B - 1
            for t in range(6):
                weigh(b, 1, t + PAIRS - 6, False)
                if t == 0:
                    pe.wait_ge(out_taken, b)
                    turn_maxima(b, 1)
                if t < 5:
                    key_scores(b, 1, t + PAIRS - 5, False)
            select(b)
            turn(b)
            project(b)

        @block.scalar
        def _(act):
            def exps(b, t, first):
                n = PAIRS * b + t
                act.wait_ge(t_done, n + 1)
                if not (first and t < 2):
                    act.wait_ge(pv_done, n - 1)
                act.activation(pT[:, t % 2, :].rearrange("p (k w) -> p k w", k=SB), sT_ps[0:KC, :, 0:TB * ROWS], ACT.Exp).then_inc(p_ready, 1)

            def take_keys(b, u):
                act.wait_ge(k_done, SB * b + u + 1)
                if u == 2 or not (isinstance(b, int) and b == 0):
                    act.wait_ge(k2_ready, SB * b + u // 2)
                act.activation(krest[:, u % 2, :], misc_ps[:, 0:SW], ACT.Identity, bias=bias[:, 1:2]).then_inc(k32_ready, 1)

            def take_values(b, s, u):
                act.wait_ge(v_done, SB * b + u + 1)
                act.activation(vx[:, s, u * VJ:(u + 1) * VJ, :, 0:2 * DH], misc_ps[0:KC, :].rearrange("k (j p d) -> k j p d", p=PAIRS, d=2 * DH), ACT.Copy).then_inc(v_ready, 1)

            def take_queries(b, s):
                act.wait_ge(qpack_done, b + 1)
                for hh in range(2):
                    act.activation(qpack[0:PARTS, s, :, hh, :], misc_ps[0:PARTS, 0:PAIRS * T].rearrange("x (p q) -> x p q", q=T), ACT.Copy, scale=res["slothead"][:, hh:hh + 1]).then_inc(qpack_ready, 1)

            def take_maxima(b, s, g):
                act.wait_ge(mT_done, 2 * b + g + 1)
                act.activation(qpack[PARTS:DEPTH, s, g * HALF:(g + 1) * HALF, :, :].rearrange("x p h q -> x (p h q)"), misc_ps[PARTS:DEPTH, 0:HALF * ROWS], ACT.Copy).then_inc(mT_ready, 1)

            def take_pv(b, half):
                act.wait_ge(pv_done, PAIRS * b + HALF * (half + 1))
                act.activation(pv_sb[:, half, :], pv_ps[:, 0:4 * ROWS], ACT.Copy).then_inc(pv_taken, 1)

            def take_turned(b):
                act.wait_ge(turn_done, b + 1)
                act.activation(oT[:, 0:T], misc_ps[:, 0:T], ACT.Identity, bias=bias[:, 3:4])
                act.activation(oT[:, T:ROWS], misc_ps[:, T:ROWS], ACT.Copy).then_inc(oT_ready, 1)

            def take_out(b):
                act.wait_ge(out_done, b + 1)
                act.activation(UPD[:, bass.ds(b * T, T)], misc_ps[:, 0:T], ACT.Identity, bias=bias[:, 2:3]).then_inc(out_taken, 1)

            def batch(i, s, first, last):
                b = 2 * i + s
                for t in range(PAIRS):
                    if t < SB and not last:
                        take_keys(b + 1, t)
                    if t == 3 or t == 4:
                        take_values(b, s, t - 2)
                    if t == 5 and not last:
                        take_queries(b + 1, 1 - s)
                    if t == 7 and not first:
                        take_out(b - 1)
                    if t == 1 and not first:
                        take_pv(b - 1, 0)
                    if t == 5 and not first:
                        take_pv(b - 1, 1)
                    if t == 0 and not first:
                        take_maxima(b - 1, 1 - s, 1)
                    if t == 1:
                        take_values(b, s, 0)
                    if t == 4:
                        take_maxima(b, s, 0)
                    if t == 6 and not first:
                        take_turned(b - 1)
                    if t >= 5:
                        exps(b, t - 5, first)
                    elif not first:
                        exps(b - 1, t + PAIRS - 5, False)

            act.wait_ge(set_up, 4)
            for n in range(N):
                cols = slice(n * W, (n + 1) * W)
                act.wait_ge(q32_ready, n + 1)
                act.activation(qpart[:, 0, cols], q32[:, cols], ACT.Copy).then_inc(q0_ready, 1)
                act.wait_ge(qrest_ready, n + 1)
                act.activation(qpart[:, 1, cols], q32[:, cols], ACT.Copy).then_inc(q1_ready, 1)
            for u in range(SB):
                take_keys(0, u)
            take_queries(0, 0)
            over_batches(act, batch)
            b = B - 1
            for t in range(5):
                if t == 0:
                    take_maxima(b, 1, 1)
                if t == 1:
                    take_pv(b, 0)
                exps(b, t + PAIRS - 5, False)
            take_pv(b, 1)
            take_turned(b)
            take_out(b)

        @block.vector
        def _(dve):
            def take_scores(b, s, t):
                dve.wait_ge(s_done, PAIRS * b + t + 1)
                out3 = scratch[:, :].rearrange("r (k w) -> r k w", k=SB)
                if masked:
                    if t == 0:
                        dve.wait_ge(mask_ready, b + 1)
                    dve.memset(carrier[:, :], 0.0)
                    m3 = maskb[:, s, :].bitcast(F32).rearrange("r (k w) -> r k w", k=SB)
                    dve.tensor_tensor_reduce(out3, score_ps[0:ROWS, :, 0:SW], m3, 1.0, -3.0e38, ALU.add, ALU.max, mx[:, t:t + 1]).then_inc(s_taken, 1)
                else:
                    dve.tensor_reduce(mx[:, t:t + 1], score_ps[0:ROWS, :, 0:SW], AX.XY, ALU.max).then_inc(s_taken, 1)

            def split_maxima(b, g):
                cols = slice(g * HALF, (g + 1) * HALF)
                n = 2 * b + g + 1
                dve.wait_ge(s_taken, PAIRS * b + (g + 1) * HALF)
                if masked:
                    dve.tensor_scalar(rowlive[:, :], mx[:, cols], MASKED / 2, None, ALU.is_gt).then_inc(rowlive_ready, 1)
                    dve.wait_ge(rowlive_ready, n)
                    dve.scalar_tensor_tensor(nmax[:, :], mx[:, cols], -1.0, rowlive[:, :], ALU.mult, ALU.mult).then_inc(nmax_ready, 1)
                    dve.wait_ge(nmax_ready, n)
                    dve.tensor_copy(mpart[:, cols, 0], nmax[:, :]).then_inc(nmax_step, 1)
                    dve.wait_ge(nmax_step, n)
                    dve.tensor_tensor(mpart[:, cols, 1], nmax[:, :], mpart[:, cols, 0], ALU.subtract).then_inc(mpart_ready, 1)
                else:
                    dve.tensor_scalar(mpart[:, cols, 0], mx[:, cols], -1.0, None, ALU.mult).then_inc(nmax_step, 1)
                    dve.wait_ge(nmax_step, n)
                    dve.scalar_tensor_tensor(mpart[:, cols, 1], mx[:, cols], -1.0, mpart[:, cols, 0], ALU.mult, ALU.subtract).then_inc(mpart_ready, 1)

            def split_keys(b, u, before):
                part = kpart[:, 0, u * SW:(u + 1) * SW]
                dve.wait_ge(k32_ready, SB * b + u + 1)
                if u == 0 and before is not None:
                    s, count = before
                    for half in range(2):
                        dve.wait_ge(kpack_dma[s][half], count)
                dve.tensor_copy(part, krest[:, u % 2, :]).then_inc(k0_ready, 1)
                dve.wait_ge(k0_ready, SB * b + u + 1)
                dve.tensor_tensor(krest[:, u % 2, :], krest[:, u % 2, :], part, ALU.subtract).then_inc(krest_ready, 1)

            def find_live(b):
                dve.wait_ge(live_done, b + 1)
                if not (isinstance(b, int) and b == 0):
                    dve.wait_ge(pen_ready, b)
                dve.tensor_scalar(live[:, :], misc_ps[:, 0:T], MASKED * (KEYS - 0.5), None, ALU.is_gt).then_inc(live_ready, 1)
                dve.wait_ge(live_ready, b + 1)
                dve.tensor_tensor(qlive[:, :, :], qpart[:, :, bass.ds(b * T, T)], live[:, :].unsqueeze(1).to_broadcast([C, 3, T]), ALU.mult).then_inc(qlive_ready, 1)

            def normalise(b):
                dve.wait_ge(sel_done, b + 1)
                sel = misc_ps[0:ROWS, 0:PAIRS * VD].rearrange("r (p d) -> r p d", d=VD)
                dve.reciprocal(rrow[:, :], sel[:, :, 2 * DH]).then_inc(recip_ready, 1)
                own = res["rowsel"][0:ROWS, :].unsqueeze(1).to_broadcast([ROWS, PAIRS, 2 * DH])
                dve.tensor_tensor(o_sel[:, :, :], sel[:, :, 0:2 * DH], own, ALU.mult).then_inc(osel_ready, 1)
                dve.wait_ge(recip_ready, b + 1)
                dve.wait_ge(osel_ready, b + 1)
                dve.tensor_tensor(o_nrm[:, :, :], o_sel[:, :, :], rrow[:, :].unsqueeze(2).to_broadcast([ROWS, PAIRS, 2 * DH]), ALU.mult).then_inc(onrm_ready, 1)

            def batch(i, s, first, last):
                b = 2 * i + s
                for t in range(PAIRS):
                    if t == 6 and not first:
                        normalise(b - 1)
                    take_scores(b, s, t)
                    if t < SB and not last:
                        split_keys(b + 1, t, (s, 16 * SLOTS * (i + 1)))
                    if t % HALF == HALF - 1:
                        split_maxima(b, t // HALF)
                    if t == 3 and masked and not last:
                        find_live(b + 1)

            dve.wait_ge(w_dma, 16 * 5)
            for n in range(N):
                dve.wait_ge(q_done, n + 1)
                cols = slice(n * W, (n + 1) * W)
                dve.tensor_scalar(q32[:, cols], misc_ps[:, 0:W], bias[:, 0:1], float(DH) ** -0.5, ALU.add, ALU.mult).then_inc(q32_ready, 1)
                dve.wait_ge(q0_ready, n + 1)
                dve.tensor_tensor(q32[:, cols], q32[:, cols], qpart[:, 0, cols], ALU.subtract).then_inc(qrest_ready, 1)
                dve.wait_ge(qrest_ready, n + 1)
                dve.wait_ge(q1_ready, n + 1)
                dve.tensor_tensor(qpart[:, 2, cols], q32[:, cols], qpart[:, 1, cols], ALU.subtract).then_inc(q2_ready, 1)
            for u in range(SB):
                split_keys(0, u, None)
            if masked:
                find_live(0)
            over_batches(dve, batch)
            normalise(B - 1)


def rms_phase(nc, res, src, dst, w, ph):
    W, N = chunks_of(res["tokens"])
    with ExitStack() as ctx:
        sem = phase_semaphores(nc, ctx, ph)
        sq = ctx.enter_context(nc.sbuf_tensor(ph + "sq", [C, N, W], F32))
        sd = ctx.enter_context(nc.sbuf_tensor(ph + "sd", [C, N, W], F32))
        ms_ps = ctx.enter_context(nc.psum_tensor(ph + "ms", [C, N, 512], F32))
        sq_ready = sem("sq_ready")
        ms_done = sem("ms_done")
        sd_ready = sem("sd_ready")
        rrms_ready = sem("rrms_ready")
        dst_ready = sem("dst_ready")
        block = ctx.enter_context(nc.Block())

        @block.tensor
        def _(pe):
            for n in range(N):
                pe.wait_ge(sq_ready, n + 1)
                pe.matmul(ms_ps[:, n, 0:W], res["avg"][:, :], sq[:, n, :], start=True, stop=True).then_inc(ms_done, 1)

        @block.scalar
        def _(act):
            for n in range(N):
                act.activation(sq[:, n, :], src[:, n * W:(n + 1) * W], ACT.Square).then_inc(sq_ready, 1)
            for n in range(N):
                act.wait_ge(ms_done, n + 1)
                act.activation(sd[:, n, :], ms_ps[:, n, 0:W], ACT.Sqrt, bias=res["eps"][:, 0:1]).then_inc(sd_ready, 1)

        @block.vector
        def _(dve):
            for n in range(N):
                dve.wait_ge(sd_ready, n + 1)
                dve.reciprocal(sd[:, n, :], sd[:, n, :]).then_inc(rrms_ready, 1)
                dve.wait_ge(rrms_ready, n + 1)
                dve.scalar_tensor_tensor(dst[:, n * W:(n + 1) * W], src[:, n * W:(n + 1) * W], w, sd[:, n, :], ALU.mult, ALU.mult).then_inc(dst_ready, 1)


class Steps:

    def __init__(self, eng, sem):
        self.eng, self.sem, self.n = eng, sem, 0

    def __call__(self, ins):
        self.n += 1
        ins.then_inc(self.sem, 1)
        self.eng.wait_ge(self.sem, self.n)


def top_two(dve, step, values, best, where, wheref, iota, one_hot):
    rows, tiles = values.shape[0], values.shape[1]
    for t in range(tiles):
        step(dve.max(best[:, t, :], values[:, t, :]))
        step(dve.max_index(where[:, t, :], best[:, t, :], values[:, t, :]))
    step(dve.tensor_copy(wheref, where))
    io = iota.unsqueeze(1).to_broadcast([rows, tiles, E])
    for k in range(2):
        step(dve.tensor_tensor(one_hot[:, k, :, :], io, wheref[:, :, k:k + 1].to_broadcast([rows, tiles, E]), ALU.is_equal))


def moe_phase(nc, res, w, ph):
    HN, UPD = res["HN"], res["UPD"]
    tokens = res["tokens"]
    NT = tokens // ROWS
    W, N = chunks_of(tokens)
    G = E // 2 + 1
    units = [(n, q) for n in range(N) for q in range(G)]
    with ExitStack() as ctx:
        sem = phase_semaphores(nc, ctx, ph)
        sb = lambda n, s, d=F32: ctx.enter_context(nc.sbuf_tensor(ph + n, s, d))
        pb = lambda n, s: ctx.enter_context(nc.psum_tensor(ph + n, s, F32))
        wg = sb("wg", [C, G, C])
        wu = sb("wu", [C, G, C])
        wd = sb("wd", [C, G, C])
        wgate = sb("wgate", [C, E])
        ebias = sb("ebias", [ROWS, E])
        iota = sb("iota", [ROWS, E])
        probs = sb("probs", [ROWS, NT, E])
        stat = sb("stat", [ROWS, NT])
        best = sb("best", [ROWS, NT, 8])
        where = sb("where", [ROWS, NT, 8], U32)
        wheref = sb("wheref", [ROWS, NT, 8])
        one_hot = sb("one_hot", [ROWS, 2, NT, E])
        comb = sb("comb", [ROWS, NT, E + 1])
        comb_wide = sb("comb_wide", [ROWS, NT, (E + 1) * I0])
        sg = sb("sg", [C, 2, W])
        hid = sb("hid", [C, 2, W])
        g_ps = pb("g_ps", [C, 2, 512])
        u_ps = pb("u_ps", [C, 2, 512])
        c_ps = pb("c_ps", [C, 2, 512])
        y_ps = pb("y_ps", [C, 512])
        r_ps = pb("r_ps", [C, 512])
        w_dma = sem("w_dma")
        logits_done = sem("logits_done")
        max_off = sem("max_off")
        exp_ready = sem("exp_ready")
        route = sem("route")
        comb_ready = sem("comb_ready")
        wide_ready = sem("wide_ready")
        g_done = sem("g_done")
        sg_ready = sem("sg_ready")
        c_done = sem("c_done")
        hu_ready = sem("hu_ready")
        hid_ready = sem("hid_ready")
        y_done = sem("y_done")
        y_taken = sem("y_taken")
        block = ctx.enter_context(nc.Block())
        weights = [(wgate, w["wgate"]), (ebias, w["ebias"]), (iota, w["iota"]), (wg, w["wg"]), (wu, w["wu"]), (wd, w["wd"])]
        NW = 16 * len(weights)

        def width(q):
            return C if q < G - 1 else I0

        @block.sync
        def _(sp):
            for dst, src in weights:
                sp.dma_start(dst[tuple(slice(None) for _ in dst.shape)], src).then_inc(w_dma, 16)

        @block.tensor
        def _(pe):
            pe.wait_ge(w_dma, NW)
            for t in range(NT):
                mm = pe.matmul(r_ps[0:ROWS, t * E:(t + 1) * E], HN[:, t * ROWS:(t + 1) * ROWS], wgate[:, :], start=True, stop=True)
            mm.then_inc(logits_done, 1)

            def down(k):
                n, q = units[k]
                m = width(q)
                pe.wait_ge(hid_ready, k + 1)
                if q == 0 and n:
                    pe.wait_ge(y_taken, n)
                pe.matmul(y_ps[:, 0:W], wd[0:m, q, :], hid[0:m, k % 2, :], start=(q == 0), stop=(q == G - 1)).then_inc(y_done, 1)

            for k, (n, q) in enumerate(units):
                m = width(q)
                x = HN[:, n * W:(n + 1) * W]
                if k >= 2:
                    pe.wait_ge(hu_ready, k - 1)
                pe.matmul(g_ps[0:m, k % 2, 0:W], wg[:, q, 0:m], x, start=True, stop=True)
                pe.matmul(u_ps[0:m, k % 2, 0:W], wu[:, q, 0:m], x, start=True, stop=True).then_inc(g_done, 1)
                if k >= 2:
                    pe.wait_ge(hid_ready, k - 1)
                for tt in range(W // ROWS):
                    tile = n * (W // ROWS) + tt
                    if q == 0:
                        pe.wait_ge(wide_ready, tile + 1)
                    wide = comb_wide[:, tile, q * C:q * C + m]
                    mm = pe.transpose(c_ps[0:m, k % 2, tt * ROWS:(tt + 1) * ROWS], wide, res["ident"][0:ROWS, 0:ROWS])
                mm.then_inc(c_done, 1)
                if k:
                    down(k - 1)
            down(len(units) - 1)

        @block.gpsimd
        def _(pool):
            pool.wait_ge(comb_ready, 1)
            for t in range(NT):
                pool.tensor_copy(comb_wide[:, t, :].rearrange("r (e i) -> r e i", i=I0), comb[:, t, :].unsqueeze(2).to_broadcast([ROWS, E + 1, I0])).then_inc(wide_ready, 1)

        @block.scalar
        def _(act):
            act.wait_ge(max_off, 1)
            act.activation(probs[:, :, :], probs[:, :, :], ACT.Exp).then_inc(exp_ready, 1)
            for k, (n, q) in enumerate(units):
                m = width(q)
                act.wait_ge(g_done, k + 1)
                if k >= 2:
                    act.wait_ge(hu_ready, k - 1)
                act.activation(sg[0:m, k % 2, :], g_ps[0:m, k % 2, 0:W], ACT.Silu).then_inc(sg_ready, 1)

        @block.vector
        def _(dve):
            step = Steps(dve, route)
            each = lambda v: v.unsqueeze(2).to_broadcast([ROWS, NT, E])
            dve.wait_ge(w_dma, NW)
            dve.wait_ge(logits_done, 1)
            step(dve.tensor_tensor(probs[:, :, :], r_ps[0:ROWS, 0:NT * E].rearrange("r (t e) -> r t e", e=E), ebias[:, :].unsqueeze(1).to_broadcast([ROWS, NT, E]), ALU.add))
            step(dve.tensor_reduce(stat[:, :], probs[:, :, :], AX.X, ALU.max))
            dve.tensor_tensor(probs[:, :, :], probs[:, :, :], each(stat[:, :]), ALU.subtract).then_inc(max_off, 1)
            dve.wait_ge(exp_ready, 1)
            step(dve.tensor_reduce(stat[:, :], probs[:, :, :], AX.X, ALU.add))
            step(dve.reciprocal(stat[:, :], stat[:, :]))
            step(dve.tensor_tensor(probs[:, :, :], probs[:, :, :], each(stat[:, :]), ALU.mult))
            top_two(dve, step, probs[:, :, :], best[:, :, :], where[:, :, :], wheref[:, :, :], iota[:, :], one_hot[:, :, :, :])
            step(dve.tensor_tensor(stat[:, :], best[:, :, 0], best[:, :, 1], ALU.add))
            step(dve.reciprocal(stat[:, :], stat[:, :]))
            step(dve.tensor_tensor(one_hot[:, 0, :, :], one_hot[:, 0, :, :], one_hot[:, 1, :, :], ALU.add))
            step(dve.tensor_tensor(probs[:, :, :], probs[:, :, :], one_hot[:, 0, :, :], ALU.mult))
            step(dve.memset(comb[:, :, E:E + 1], 1.0))
            dve.tensor_tensor(comb[:, :, 0:E], probs[:, :, :], each(stat[:, :]), ALU.mult).then_inc(comb_ready, 1)

            def take(n):
                dve.wait_ge(y_done, (n + 1) * G)
                cols = slice(n * W, (n + 1) * W)
                dve.tensor_tensor(UPD[:, cols], UPD[:, cols], y_ps[:, 0:W], ALU.add).then_inc(y_taken, 1)

            for k, (n, q) in enumerate(units):
                m = width(q)
                dve.wait_ge(sg_ready, k + 1)
                if k >= 2:
                    dve.wait_ge(y_done, k - 1)
                dve.tensor_tensor(hid[0:m, k % 2, :], sg[0:m, k % 2, :], u_ps[0:m, k % 2, 0:W], ALU.mult).then_inc(hu_ready, 1)
                dve.wait_ge(hu_ready, k + 1)
                dve.wait_ge(c_done, k + 1)
                dve.tensor_tensor(hid[0:m, k % 2, :], hid[0:m, k % 2, :], c_ps[0:m, k % 2, 0:W], ALU.mult).then_inc(hid_ready, 1)
                if q == 0 and n:
                    take(n - 1)
            take(N - 1)


def expert_ffn_phase(nc, res, w, ph):
    XN, UPD = res["XN"], res["UPD"]
    tokens, B = res["tokens"], res["B"]
    W, N = chunks_of(tokens)
    BW = W // T
    with ExitStack() as ctx:
        sem = phase_semaphores(nc, ctx, ph)
        sb = lambda n, s, d=F32: ctx.enter_context(nc.sbuf_tensor(ph + n, s, d))
        pb = lambda n, s: ctx.enter_context(nc.psum_tensor(ph + n, s, F32))
        w1 = sb("w1", [C, E, F1])
        w2 = sb("w2", [C, E, FB, C])
        b1 = sb("b1", [C, E, FB])
        b2 = sb("b2", [C, E])
        wr = sb("wr", [C, E])
        iota = sb("iota", [C, E])
        ones = sb("ones", [B, C])
        pooled = sb("pooled", [C, B])
        lg = sb("lg", [B, 1, E])
        best = sb("best", [B, 1, 8])
        where = sb("where", [B, 1, 8], U32)
        wheref = sb("wheref", [B, 1, 8])
        one_hot = sb("one_hot", [B, 2, 1, E])
        wt = sb("wt", [B, 4])
        comb = sb("comb", [B, E])
        diag = sb("diag", [B, E, B])
        cw = sb("cw", [C, E, B])
        hs = sb("hs", [C, 2, FB, W])
        part = sb("part", [C, 2, W])
        h_ps = pb("h_ps", [C, FB, 512])
        y_ps = pb("y_ps", [C, 2, 512])
        r_ps = pb("r_ps", [C, 512])
        w_dma = sem("w_dma")
        route = sem("route")
        pooled_ready = sem("pooled_ready")
        logits_done = sem("logits_done")
        diff_ready = sem("diff_ready")
        exp_ready = sem("exp_ready")
        diag_ready = sem("diag_ready")
        spread = sem("spread")
        cw_ready = sem("cw_ready")
        h_done = sem("h_done")
        hs_ready = sem("hs_ready")
        y_done = sem("y_done")
        y_taken = sem("y_taken")
        added = sem("added")
        block = ctx.enter_context(nc.Block())
        small = [(wr, w["wr"]), (iota, w["iota1"]), (b1, w["b1"]), (b2, w["b2"])]
        NW = 16 * (len(small) + 2)

        @block.sync
        def _(sp):
            for dst, src in small + [(w1, w["w1"]), (w2, w["w2"])]:
                sp.dma_start(dst[tuple(slice(None) for _ in dst.shape)], src).then_inc(w_dma, 16)

        def over_chunks(eng, chunk):
            chunk(0, True)
            if N > 1:
                with eng.Fori(1, N) as n:
                    chunk(n, False)

        @block.tensor
        def _(pe):
            pe.wait_ge(w_dma, NW)
            pe.wait_ge(pooled_ready, 1)
            pe.matmul(r_ps[0:B, 0:E], pooled[:, :], wr[:, :], start=True, stop=True).then_inc(logits_done, 1)
            pe.wait_ge(diag_ready, 1)
            pe.matmul(r_ps[:, 0:E * B], ones[:, :], diag[:, :, :].rearrange("b e c -> b (e c)"), start=True, stop=True).then_inc(spread, 1)

            def up(n, e, first):
                x = XN[:, bass.ds(n * W, W)]
                for f in range(FB):
                    if not (first and e == 0):
                        pe.wait_ge(hs_ready, FB * (E * n + e - 1) + f + 1)
                    pe.matmul(h_ps[:, f, 0:W], w1[:, e, f * C:(f + 1) * C], x, start=True, stop=True).then_inc(h_done, 1)

            def down(n, e, first):
                pe.wait_ge(hs_ready, FB * (E * n + e) + FB)
                if not (first and e < 2):
                    pe.wait_ge(y_taken, E * n + e - 1)
                for f in range(FB):
                    mm = pe.matmul(y_ps[:, e % 2, 0:W], w2[:, e, f, :], hs[:, e % 2, f, :], start=(f == 0), stop=(f == FB - 1))
                mm.then_inc(y_done, 1)

            def chunk(n, first):
                for e in range(E):
                    up(n, e, first)
                    if e:
                        down(n, e - 1, first)
                    elif not first:
                        down(n - 1, E - 1, False)

            over_chunks(pe, chunk)
            down(N - 1, E - 1, False)

        @block.scalar
        def _(act):
            act.wait_ge(diff_ready, 1)
            act.activation(wt[:, 0:1], wt[:, 0:1], ACT.Exp).then_inc(exp_ready, 1)
            act.wait_ge(w_dma, NW)

            def chunk(n, first):
                for e in range(E):
                    for f in range(FB):
                        act.wait_ge(h_done, FB * (E * n + e) + f + 1)
                        if f == 0 and not (first and e < 2):
                            act.wait_ge(y_done, E * n + e - 1)
                        act.activation(hs[:, e % 2, f, :], h_ps[:, f, 0:W], ACT.Gelu, bias=b1[:, e, f:f + 1]).then_inc(hs_ready, 1)

            over_chunks(act, chunk)

        @block.vector
        def _(dve):
            step = Steps(dve, route)
            step(dve.memset(ones[:, :], 1.0))
            step(dve.memset(wt[:, :], 0.0))
            step(dve.tensor_reduce(pooled[:, :], XN[:, :].rearrange("c (b t) -> c b t", t=T), AX.X, ALU.add))
            dve.tensor_scalar(pooled[:, :], pooled[:, :], 1.0 / T, None, ALU.mult).then_inc(pooled_ready, 1)
            dve.wait_ge(w_dma, NW)
            dve.wait_ge(logits_done, 1)
            step(dve.tensor_copy(lg[:, 0, :], r_ps[0:B, 0:E]))
            top_two(dve, step, lg[:, :, :], best[:, :, :], where[:, :, :], wheref[:, :, :], iota[0:B, :], one_hot[:, :, :, :])
            dve.tensor_tensor(wt[:, 0:1], best[:, 0, 1:2], best[:, 0, 0:1], ALU.subtract).then_inc(diff_ready, 1)
            dve.wait_ge(exp_ready, 1)
            step(dve.tensor_scalar(wt[:, 1:2], wt[:, 0:1], 1.0, None, ALU.add))
            step(dve.reciprocal(wt[:, 2:3], wt[:, 1:2]))
            step(dve.tensor_tensor(wt[:, 3:4], wt[:, 0:1], wt[:, 2:3], ALU.mult))
            step(dve.tensor_scalar(comb[:, :], one_hot[:, 0, 0, :], wt[:, 2:3], None, ALU.mult))
            step(dve.scalar_tensor_tensor(comb[:, :], one_hot[:, 1, 0, :], wt[:, 3:4], comb[:, :], ALU.mult, ALU.add))
            dve.tensor_tensor(diag[:, :, :], comb[:, :].unsqueeze(2).to_broadcast([B, E, B]), res["ident"][0:B, 0:B].unsqueeze(1).to_broadcast([B, E, B]), ALU.mult).then_inc(diag_ready, 1)
            dve.wait_ge(spread, 1)
            dve.tensor_copy(cw[:, :, :], r_ps[:, 0:E * B].rearrange("c (e b) -> c e b", b=B)).then_inc(cw_ready, 1)
            dve.wait_ge(cw_ready, 1)

            def chunk(n, first):
                cols = bass.ds(n * W, W)
                for e in range(E):
                    k = E * n + e
                    dve.wait_ge(y_done, k + 1)
                    weight = cw[:, e, bass.ds(n * BW, BW)].unsqueeze(2).to_broadcast([C, BW, T])
                    y3 = y_ps[:, e % 2, 0:W].rearrange("c (b t) -> c b t", t=T)
                    dst = UPD[:, cols] if e == 0 else part[:, e % 2, :]
                    if e >= 2:
                        dve.wait_ge(added, (E - 1) * n + e - 2)
                    dve.scalar_tensor_tensor(dst.rearrange("c (b t) -> c b t", t=T), y3, b2[:, e:e + 1], weight, ALU.add, ALU.mult).then_inc(y_taken, 1)
                    dve.wait_ge(y_taken, k + 1)
                    if e:
                        if e >= 2:
                            dve.wait_ge(added, (E - 1) * n + e - 1)
                        dve.tensor_tensor(UPD[:, cols], UPD[:, cols], part[:, e % 2, :], ALU.add).then_inc(added, 1)

            over_chunks(dve, chunk)


def store_phase(nc, res, gate, out, ph):
    XT, UPD = res["XT"], res["UPD"]
    W, N = chunks_of(res["tokens"])
    with ExitStack() as ctx:
        sem = phase_semaphores(nc, ctx, ph)
        x_ready = sem("x_ready")
        stored = sem("stored")
        block = ctx.enter_context(nc.Block())

        @block.vector
        def _(dve):
            for n in range(N):
                cols = slice(n * W, (n + 1) * W)
                dve.scalar_tensor_tensor(XT[:, cols], UPD[:, cols], gate, XT[:, cols], ALU.mult, ALU.add).then_inc(x_ready, 1)

        @block.sync
        def _(sp):
            for n in range(N):
                sp.wait_ge(x_ready, n + 1)
                sp.dma_start(out[:, n * W:(n + 1) * W], XT[:, n * W:(n + 1) * W]).then_inc(stored, 16)
            sp.wait_ge(stored, 16 * N)


def self_attention_phase(nc, res, w, ph):
    XN, HN, UPD = res["XN"], res["HN"], res["UPD"]
    NT = res["B"] // 2
    with ExitStack() as ctx:
        sem = phase_semaphores(nc, ctx, ph)
        sb = lambda n, s, d=F32: ctx.enter_context(nc.sbuf_tensor(ph + n, s, d))
        pb = lambda n, s: ctx.enter_context(nc.psum_tensor(ph + n, s, F32))
        wcos = sb("wcos", [C, PAIRS + 1, C])
        wsin = sb("wsin", [C, PAIRS + 1, C])
        wqn = sb("wqn", [2 * NOPE, PAIRS, C])
        wkvb = sb("wkvb", [2 * NOPE, PAIRS, 2 * RANK])
        wo = sb("wo", [2 * NOPE, PAIRS, C])
        wlat = sb("wlat", [C, 2 * RANK])
        tabs = sb("tabs", [C, 2, T])
        causal = sb("causal", [C, T])
        latsel = sb("latsel", [ROWS, 2 * RANK])
        wout = sb("wout", [C, 2, C])
        hs2 = sb("hs2", [C, 2, 2, 2, T])
        tc_ = sb("tc", [C, 2, 4, ROWS])
        ts_ = sb("ts", [C, 2, 4, ROWS])
        tck = sb("tck", [C, ROWS])
        tsk = sb("tsk", [C, ROWS])
        qp = sb("qp", [C, 2, PAIRS, ROWS + 8])
        kblk = sb("kblk", [C, 2, 2, ROWS])
        causalb = sb("causalb", [C, T], BF16)
        latb = sb("latb", [ROWS, 2, 2, 2 * RANK])
        s_sb = sb("s_sb", [C, 2, HF * T])
        mx = sb("mx", [C, 2, HF])
        rs = sb("rs", [C, 2, HF])
        pT = sb("pT", [ROWS, 2, PAIRS * C])
        uT = sb("uT", [C, 2, 2 * ROWS])
        proj_ps = pb("proj_ps", [C, 4, 512])
        key_ps = pb("key_ps", [C, 512])
        s_ps = pb("s_ps", [C, 2, 512])
        u_ps = pb("u_ps", [C, 512])

        w_dma = sem("w_dma")
        zeroed = sem("zeroed")
        fold_done = sem("fold_done")
        folded = sem("folded")
        causal_ready = sem("causal_ready")
        hs_ready = sem("hs_ready")
        proj_done = sem("proj_done")
        key_done = sem("key_done")
        rot_a = sem("rot_a")
        rot_b = sem("rot_b")
        q_ready = sem("q_ready")
        rot_k = sem("rot_k")
        lat_ready = sem("lat_ready")
        k_ready = sem("k_ready")
        s_done = sem("s_done")
        mx_ready = sem("mx_ready")
        sub_ready = sem("sub_ready")
        e_ready = sem("e_ready")
        sum_ready = sem("sum_ready")
        rec_ready = sem("rec_ready")
        p_ready = sem("p_ready")
        pT_done = sem("pT_done")
        pT_ready = sem("pT_ready")
        u_done = sem("u_done")
        u_ready = sem("u_ready")
        out_done = sem("out_done")
        out_taken = sem("out_taken")
        block = ctx.enter_context(nc.Block())
        weights = [(wcos, w["wcos"]), (wsin, w["wsin"]), (wqn, w["wqn"]), (wkvb, w["wkvb"]), (wo, w["wo0"]),
                   (wlat, w["wlat"]), (tabs, w["tabs"]), (causal, w["causal"]), (latsel, w["latsel"])]
        NW = 16 * len(weights)

        def over_slots(eng, slot):
            for i in range(min(2, NT // 2)):
                slot(i, 0)
                slot(i, 1)
            if NT > 4:
                with eng.Fori(2, NT // 2) as i:
                    slot(i, 0)
                    slot(i, 1)
            slot(NT // 2, 0)
            slot(NT // 2, 1)
            slot(NT // 2 + 1, 0)
            slot(NT // 2 + 1, 1)

        def exists(n):
            return not isinstance(n, int) or 0 <= n < NT

        def wait(eng, sem, value):
            if not isinstance(value, int) or value > 0:
                eng.wait_ge(sem, value)

        @block.sync
        def _(sp):
            for dst, src in weights:
                sp.dma_start(dst[tuple(slice(None) for _ in dst.shape)], src).then_inc(w_dma, 16)

        @block.gpsimd
        def _(pool):
            pool.memset(qp[:, :, :, :], 0.0).then_inc(zeroed, 1)
            pool.memset(kblk[:, :, :, :], 0.0).then_inc(zeroed, 1)
            pool.wait_ge(zeroed, 2)

            def add_queries(m, s, half):
                pool.wait_ge(rot_b, 2 * m + half + 1)
                g = 4 * (1 - half)
                pool.tensor_tensor(qp[:, s, g:g + 4, 0:ROWS], tc_[:, half, :, :], ts_[:, half, :, :], ALU.add).then_inc(q_ready, 1)

            def slot(i, s):
                m = 2 * i + s
                if exists(m):
                    pool.wait_ge(rot_k, 2 * m + 2)
                    wait(pool, s_done, m - 1)
                    wait(pool, q_ready, 2 * m)
                    for b in range(2):
                        for hh in range(2):
                            half = slice(64 * hh, 64 * hh + 64)
                            pool.tensor_tensor(kblk[half, s, b, hh * T:hh * T + T], tck[half, b * T:b * T + T], tsk[half, b * T:b * T + T], ALU.add).then_inc(k_ready, 1)
                    pool.wait_ge(k_ready, 4 * m + 4)
                    add_queries(m, s, 0)
                if exists(m - 2):
                    s3 = s_sb[:, s, :].rearrange("q (h t) -> q h t", t=T)
                    pool.wait_ge(rec_ready, m - 1)
                    pool.tensor_tensor(s3, s3, rs[:, s, :].unsqueeze(2).to_broadcast([C, HF, T]), ALU.mult).then_inc(p_ready, 1)
                if exists(m):
                    add_queries(m, s, 1)

            over_slots(pool, slot)

        @block.tensor
        def _(pe):
            pe.wait_ge(w_dma, NW)
            for p in range(PAIRS):
                pe.matmul(key_ps[:, p * 2 * RANK:(p + 1) * 2 * RANK], wqn[:, p, :], wkvb[:, p, :], start=True, stop=True)
            for p in range(PAIRS):
                g = 32 * (p % 4)
                mm = pe.matmul(u_ps[g:g + 32, (p // 4) * C:(p // 4 + 1) * C], wkvb[:, p, :], wo[:, p, :], start=True, stop=True)
            mm.then_inc(fold_done, 1)
            pe.wait_ge(folded, 2)
            pe.wait_ge(causal_ready, 1)

            def scores(n, s):
                pe.wait_ge(q_ready, 2 * n + 2)
                pe.wait_ge(k_ready, 4 * n + 4)
                wait(pe, sub_ready, n)
                wait(pe, pT_ready, n - 1)
                for k in range(2):
                    pe.matmul(s_ps[:, k, 0:8 * T].rearrange("q (h t) -> q h t", t=T), res["identb"][:, :], causalb[:, :].unsqueeze(1).to_broadcast([C, 8, T]), start=True, stop=False)
                    for p in range(4 * k, 4 * k + 4):
                        for b in range(2):
                            mm = pe.matmul(s_ps[64 * b:64 * b + 64, k, (p % 4) * ROWS:(p % 4 + 1) * ROWS], qp[:, s, p, b * T:b * T + 64], kblk[:, s, b, :], start=False, stop=(p % 4 == 3))
                mm.then_inc(s_done, 1)

            def project(m, half):
                bank = 2 * (1 - half)
                tokens = HN[:, bass.ds(m * ROWS, ROWS)]
                for k, wt in enumerate((wcos, wsin)):
                    for pp in range(4):
                        mm = pe.matmul(proj_ps[:, bank + k, pp * ROWS:(pp + 1) * ROWS], wt[:, bank * 2 + pp, :], tokens, start=True, stop=True)
                mm.then_inc(proj_done, 1)

            def slot(i, s):
                m = 2 * i + s
                if exists(m - 2):
                    scores(m - 2, s)
                if exists(m - 4):
                    pe.wait_ge(u_ready, m - 3)
                    for pg in range(2):
                        mm = pe.matmul(u_ps[:, 256:256 + ROWS], wout[:, pg, :], uT[:, s, pg * ROWS:(pg + 1) * ROWS], start=(pg == 0), stop=(pg == 1))
                    mm.then_inc(out_done, 1)
                if exists(m):
                    wait(pe, rot_b, 2 * m - 1)
                    project(m, 0)
                    wait(pe, rot_k, 2 * m)
                if exists(m - 3):
                    pe.wait_ge(lat_ready, 2 * (m - 2))
                if exists(m):
                    for k, wt in enumerate((wcos, wsin)):
                        mm = pe.matmul(key_ps[:, k * ROWS:(k + 1) * ROWS], wt[:, PAIRS, :], HN[:, bass.ds(m * ROWS, ROWS)], start=True, stop=True)
                if exists(m - 2):
                    pe.wait_ge(hs_ready, m - 1)
                    for b in range(2):
                        mm = pe.matmul(key_ps[0:ROWS, 256 + b * 2 * RANK:256 + (b + 1) * 2 * RANK], hs2[:, s, b, :, :].rearrange("c a t -> c (a t)"), wlat[:, :], start=True, stop=True)
                if exists(m) or exists(m - 2):
                    mm.then_inc(key_done, 1)
                if exists(m - 3):
                    pe.wait_ge(p_ready, m - 2)
                    if exists(m - 2):
                        pe.wait_ge(sub_ready, m - 1)
                    elif exists(m - 4):
                        pe.wait_ge(pT_ready, m - 3)
                    for p in range(PAIRS):
                        mm = pe.transpose(s_ps[0:ROWS, p // 4, (p % 4) * C:(p % 4 + 1) * C], s_sb[:, 1 - s, p * ROWS:(p + 1) * ROWS], res["ident"][:, :])
                    mm.then_inc(pT_done, 1)
                if exists(m):
                    wait(pe, rot_b, 2 * m)
                    project(m, 1)
                if exists(m - 3):
                    pe.wait_ge(pT_ready, m - 2)
                    pe.wait_ge(lat_ready, 2 * (m - 2))
                    wait(pe, out_taken, m - 3)
                    for pg in range(2):
                        for b in range(2):
                            for g in range(4):
                                p = 4 * pg + g
                                mm = pe.matmul(u_ps[32 * g:32 * g + 32, pg * ROWS + b * T:pg * ROWS + b * T + T], latb[:, 1 - s, b, :], pT[:, 1 - s, p * C + 64 * b:p * C + 64 * b + T], start=True, stop=True)
                    mm.then_inc(u_done, 1)

            over_slots(pe, slot)

        @block.scalar
        def _(act):
            def slot(i, s):
                m = 2 * i + s
                if exists(m - 2):
                    act.wait_ge(sub_ready, m - 1)
                    act.activation(s_sb[:, s, :], s_sb[:, s, :], ACT.Exp, scale=float(NOPE + ROPE) ** -0.5).then_inc(e_ready, 1)
                if exists(m - 3):
                    act.wait_ge(pT_done, m - 2)
                    act.activation(pT[:, 1 - s, :].rearrange("r (k w) -> r k w", k=2), s_ps[0:ROWS, :, :], ACT.Copy).then_inc(pT_ready, 1)
                if exists(m - 1):
                    for b in range(2):
                        src = HN[:, bass.ds((m - 1) * ROWS + b * T, T)]
                        ins = act.activation(hs2[:, 1 - s, b, :, :], src.unsqueeze(1).to_broadcast([C, 2, T]), ACT.Copy)
                    ins.then_inc(hs_ready, 1)
                if exists(m - 3):
                    act.wait_ge(u_done, m - 2)
                    act.activation(uT[:, 1 - s, :], u_ps[:, 0:2 * ROWS], ACT.Copy).then_inc(u_ready, 1)

            over_slots(act, slot)

        @block.vector
        def _(dve):
            dve.wait_ge(w_dma, NW)
            dve.tensor_copy(causalb[:, :], causal[:, :]).then_inc(causal_ready, 1)
            dve.wait_ge(fold_done, 1)
            dve.tensor_copy(wcos[:, 0:PAIRS, :].rearrange("c p (h x) -> c p h x", h=2)[:, :, :, 0:RANK], key_ps[:, 0:PAIRS * 2 * RANK].rearrange("c (p h r) -> c p h r", h=2, r=RANK)).then_inc(folded, 1)
            dve.tensor_copy(wout[:, :, :], u_ps[:, 0:2 * C].rearrange("x (g c) -> x g c", c=C)).then_inc(folded, 1)

            def table(k, reps):
                return tabs[:, k, :].unsqueeze(1).to_broadcast([C, reps, T])

            def rotate(m, half):
                dve.wait_ge(proj_done, 2 * m + half + 1)
                wait(dve, q_ready, 2 * m - 1 + half)
                for k, (dst, done) in enumerate(((tc_, rot_a), (ts_, rot_b))):
                    src = proj_ps[:, 2 * (1 - half) + k, 0:4 * ROWS].rearrange("c (m t) -> c m t", t=T)
                    dve.tensor_tensor(dst[:, half, :, :].rearrange("c p (b t) -> c (p b) t", t=T), src, table(k, 8), ALU.mult).then_inc(done, 1)

            def slot(i, s):
                m = 2 * i + s
                s3 = s_sb[:, s, :].rearrange("q (h t) -> q h t", t=T)
                if exists(m - 2):
                    dve.wait_ge(s_done, m - 1)
                    dve.tensor_reduce(mx[:, s, :].rearrange("q (k h) -> q k h", k=2), s_ps[:, :, 0:4 * ROWS].rearrange("q k (h t) -> q k h t", t=T), AX.X, ALU.max).then_inc(mx_ready, 1)
                    wait(dve, pT_done, m - 3)
                    dve.wait_ge(mx_ready, m - 1)
                    dve.tensor_tensor(s_sb[:, s, :].rearrange("q (k h t) -> q k h t", k=2, t=T), s_ps[:, :, 0:4 * ROWS].rearrange("q k (h t) -> q k h t", t=T),
                                      mx[:, s, :].rearrange("q (k h) -> q k h", k=2).unsqueeze(3).to_broadcast([C, 2, 8, T]), ALU.subtract).then_inc(sub_ready, 1)
                if exists(m):
                    rotate(m, 0)
                if exists(m) or exists(m - 2):
                    dve.wait_ge(key_done, m + 1)
                if exists(m):
                    wait(dve, k_ready, 4 * m)
                    for k, dst in enumerate((tck, tsk)):
                        src = key_ps[:, k * ROWS:(k + 1) * ROWS].rearrange("c (b t) -> c b t", t=T)
                        dve.tensor_tensor(dst[:, :].rearrange("c (b t) -> c b t", t=T), src, table(k, 2), ALU.mult).then_inc(rot_k, 1)
                if exists(m - 2):
                    wait(dve, u_done, m - 3)
                    for b in range(2):
                        dve.tensor_tensor(latb[:, s, b, :], key_ps[0:ROWS, 256 + b * 2 * RANK:256 + (b + 1) * 2 * RANK], latsel[:, :], ALU.mult).then_inc(lat_ready, 1)
                if exists(m - 4):
                    dve.wait_ge(out_done, m - 3)
                    cols = bass.ds((m - 4) * ROWS, ROWS)
                    dve.tensor_tensor(UPD[:, cols], u_ps[:, 256:256 + ROWS], XN[:, cols], ALU.add).then_inc(out_taken, 1)
                if exists(m - 2):
                    dve.wait_ge(e_ready, m - 1)
                    dve.tensor_reduce(rs[:, s, :], s3, AX.X, ALU.add).then_inc(sum_ready, 1)
                    dve.wait_ge(sum_ready, m - 1)
                    dve.reciprocal(rs[:, s, :], rs[:, s, :]).then_inc(rec_ready, 1)
                if exists(m):
                    rotate(m, 1)

            over_slots(dve, slot)


def constants_self_attention():
    f32 = np.float32
    freqs = (f32(1.0) / f32(THETA) ** (np.arange(0, ROPE * 1, 2, dtype=f32) / f32(ROPE))).astype(f32)
    ang = np.outer(np.arange(T, dtype=f32), freqs).astype(f32)
    cos, sin = np.cos(ang).T, np.sin(ang).T
    tabs = np.zeros((C, 2, T), f32)
    for base in (0, 64):
        tabs[base:base + RANK, 0] = 1.0
        tabs[base + RANK:base + KD, 0] = np.repeat(cos, 2, axis=0)
        tabs[base + RANK:base + KD:2, 1] = -sin
        tabs[base + RANK + 1:base + KD:2, 1] = sin
    causal = np.zeros((C, T), f32)
    for base in (0, 64):
        causal[base:base + T] = np.where(np.tril(np.ones((T, T), bool)), 0.0, -1.0e30)
    r = np.arange(ROWS)
    latsel = (r[:, None] // T == np.arange(2 * RANK)[None, :] // RANK).astype(f32)
    return {"tabs": tabs, "causal": causal, "latsel": latsel}


def lay_out_self_attention(Wq, Wkva, Wkvb, Wo):
    D = NOPE + ROPE
    q = Wq.reshape(C, PAIRS, 2, D)
    swap = np.arange(ROPE) ^ 1
    z = lambda *s: np.zeros(s, np.float32)
    wcos, wsin = z(C, PAIRS + 1, 2, 64), z(C, PAIRS + 1, 2, 64)
    wcos[:, :PAIRS, :, RANK:KD] = q[..., NOPE:]
    wsin[:, :PAIRS, :, RANK:KD] = q[..., NOPE:][..., swap]
    wcos[:, PAIRS, :, 0:KD] = Wkva[:, None, :]
    wsin[:, PAIRS, :, RANK:KD] = Wkva[:, None, RANK:][..., swap]
    wqn = q[..., :NOPE].transpose(2, 3, 1, 0).reshape(2 * NOPE, PAIRS, C)
    kvb = Wkvb.reshape(RANK, PAIRS, 2, NOPE)
    wkvb = z(2, NOPE, PAIRS, 2, RANK)
    for h in range(2):
        wkvb[h, :, :, h, :] = kvb[:, :, h, :].transpose(2, 1, 0)
    wo = Wo.reshape(PAIRS, 2, D, C)[:, :, :NOPE].transpose(1, 2, 0, 3).reshape(2 * NOPE, PAIRS, C)
    lat = Wkva[:, :RANK]
    c = np.ascontiguousarray
    return {"wcos": c(wcos.reshape(C, PAIRS + 1, C)), "wsin": c(wsin.reshape(C, PAIRS + 1, C)), "wqn": c(wqn), "wkvb": c(wkvb.reshape(2 * NOPE, PAIRS, 2 * RANK)),
            "wo0": c(wo), "wlat": c(np.concatenate([lat, lat], 1))}


def constants_xattn():
    c = np.arange(C)
    d = np.arange(2 * DH)
    rowsel = ((c[:, None] // T == d[None, :] // DH) & (c[:, None] < ROWS)).astype(np.float32)
    groupsum = (c[:, None] % 32 == np.arange(2 * DH + 1)[None, :]).astype(np.float32)
    x = np.arange(SLOTS * 2 * DH)
    part = np.array(Q_PART)[x // (2 * DH)]
    qsel = (part[None, None, None, :] == np.arange(3)[None, :, None, None]) & (
        c[:, None, None, None] == np.arange(PAIRS)[None, None, :, None] * 2 * DH + (x % (2 * DH))[None, None, None, :])
    slothead = (x[:, None] // DH % 2 == np.arange(2)[None, :]).astype(np.float32)
    return {"ident": np.eye(C, dtype=np.float32), "rowsel": rowsel, "groupsum": groupsum, "slothead": slothead, "qsel": qsel.astype(np.float32)}


def lay_out_experts0(Wg, Wu, Wd, sWg, sWu, sWd):
    z = np.zeros((C, I0), np.float32)
    pair = lambda a: a.reshape(E // 2, 2, C, I0).transpose(2, 0, 1, 3).reshape(C, E // 2, C)
    up = lambda a, s: np.ascontiguousarray(np.concatenate([pair(a), np.concatenate([s[0], z], 1)[:, None]], 1))
    down = np.concatenate([Wd.reshape(E // 2, C, C).transpose(1, 0, 2), np.concatenate([sWd[0], z.T], 0)[:, None]], 1)
    return {"wg": up(Wg, sWg), "wu": up(Wu, sWu), "wd": np.ascontiguousarray(down)}


def build_program(nc, aps, out, B):
    tokens = B * T
    with ExitStack() as ctx:
        sb = lambda n, s: ctx.enter_context(nc.sbuf_tensor(n, s, F32))
        res = {"B": B, "tokens": tokens}
        for name, shape in (("XT", [C, tokens]), ("XN", [C, tokens]), ("UPD", [C, tokens]), ("HN", [C, tokens]), ("gates", [C, 4]), ("avg", [C, C]), ("eps", [C, 1]),
                            ("ident", [C, C]), ("slothead", [SLOTS * 2 * DH, 2]), ("rowsel", [C, 2 * DH]), ("groupsum", [C, 2 * DH + 1]), ("rmsw", [C, 2])):
            res[name] = sb(name, shape)
        res["identb"] = ctx.enter_context(nc.sbuf_tensor("identb", [C, C], BF16))
        res["qsel"] = ctx.enter_context(nc.sbuf_tensor("qsel", [C, 3, PAIRS, SLOTS * 2 * DH], BF16))
        gate = lambda k: res["gates"][:, k:k + 1]
        load_phase(nc, res, aps, "p0_")
        norm_phase(nc, res, None, None, "p1_")
        xattn_phase(nc, res, {k: aps[k + "_0"] for k in ("qwT", "kwT", "vwT", "owT", "bias")} | {"ctxT": aps["ctxT"], "maskT": aps["maskT"]}, aps["mask"], "p2_")
        norm_phase(nc, res, gate(0), (res["rmsw"][:, 0:1], res["HN"]), "p3_")
        self_attention_phase(nc, res, aps, "p4_")
        rms_phase(nc, res, res["UPD"], res["HN"], res["rmsw"][:, 1:2], "p5_")
        moe_phase(nc, res, aps, "p6_")
        norm_phase(nc, res, gate(2), None, "p7_")
        xattn_phase(nc, res, {k: aps[k + "_1"] for k in ("qwT", "kwT", "vwT", "owT", "bias")} | {"ctxT": aps["ctxT"]}, None, "p8_")
        norm_phase(nc, res, gate(1), None, "p9_")
        expert_ffn_phase(nc, res, aps, "p10_")
        store_phase(nc, res, gate(3), out, "p11_")


def lay_out(a):
    c = np.ascontiguousarray
    a = {k: np.asarray(v) for k, v in a.items()}
    B = a["x"].shape[0]
    o = {"xT": c(a["x"].reshape(B * T, C).T), "ctxT": c(a["ctx_1024"].transpose(0, 2, 1)), "mask": a["mask_BxSxS2_if1"]}
    o["maskT"] = c(o["mask"].transpose(0, 2, 1).reshape(B, KCH, KC, T).transpose(0, 2, 1, 3))
    o["gates"] = c(np.broadcast_to(np.concatenate([a["g_xattn"], a["g_ffn"]])[None, :], (C, 4)))
    for layer, names in ((0, ("qw", "kw", "vw", "ow", "qb", "kb", "vb", "ob")), (1, ("Wq", "Wk", "Wv", "Wo", "bq", "bk", "bv", "bo"))):
        qw, kw, vw, ow, qb, kb, vb, ob = (a[f"L{layer}_xattn_{n}"] for n in names)
        kw, kb = kw[KEY_ORDER], kb[KEY_ORDER]
        for n, m in (("qwT", qw), ("kwT", kw), ("vwT", vw), ("owT", ow)):
            o[f"{n}_{layer}"] = c(m.T)
        o[f"bias_{layer}"] = c(np.stack([qb, kb, ob, vb], 1))
    f = lambda n: a["L0_ffn_" + n]
    o["rmsw"] = c(np.stack([f("w_ln1"), f("w_ln2")], 1))
    o |= lay_out_self_attention(f("Wq"), f("Wkva"), f("Wkvb"), f("Wo"))
    o |= lay_out_experts0(f("Wg"), f("Wu"), f("Wd"), f("sWg"), f("sWu"), f("sWd"))
    o["wgate"] = f("Wgate")
    o["ebias"] = c(np.broadcast_to(f("expert_bias"), (ROWS, E)))
    o["iota"] = c(np.broadcast_to(np.arange(E, dtype=np.float32), (ROWS, E)))
    f = lambda n: a["L1_ffn_" + n]
    o["wr"] = f("Wr")
    o["iota1"] = c(np.broadcast_to(np.arange(E, dtype=np.float32), (C, E)))
    o["w1"] = c(f("W1").transpose(1, 0, 2))
    o["w2"] = c(f("W2").reshape(E, FB, C, C).transpose(2, 0, 1, 3))
    o["b1"] = c(f("b1").reshape(E, FB, C).transpose(2, 0, 1))
    o["b2"] = c(f("b2").T)
    return o | constants_xattn() | constants_self_attention()


def kernel(**inputs):
    import concourse.bacc as bacc
    from concourse.bass_utils import run_bass_kernel_spmd

    arrays = lay_out(inputs)
    B = arrays["ctxT"].shape[0]
    nc = bacc.Bacc("TRN2", target_bir_lowering=False, num_devices=1)
    aps = {k: nc.dram_tensor("in_" + k, v.shape, mybir.dt.from_np(v.dtype), kind="ExternalInput").ap() for k, v in arrays.items()}
    out = nc.dram_tensor("outT", (C, B * T), F32, kind="ExternalOutput").ap()
    build_program(nc, aps, out, B)
    got = run_bass_kernel_spmd(nc, [{"in_" + k: v for k, v in arrays.items()}], core_ids=[0]).results[0]["outT"]
    return np.ascontiguousarray(got.T).reshape(B, T, C)
```
